# Optimizing a Trainium2 kernel written in Bass

```python
import numpy as np
import jax
import jax.numpy as jnp

def _softmax(x, axis=-1):
    return jax.nn.softmax(x, axis=axis)

def _gelu(x):
    return jax.nn.gelu(x, approximate=True)

def _silu(x):
    return jax.nn.silu(x)

def _sigmoid(x):
    return jax.nn.sigmoid(x)

def _layernorm(x, axis=-1, eps=1e-05):
    m = jnp.mean(x, axis=axis, keepdims=True)
    v = jnp.var(x, axis=axis, keepdims=True)
    return (x - m) / jnp.sqrt(v + eps)

def _scatter_add(tgt, idx, src, axis=0):
    return tgt.at[idx].add(src)

def _segment_sum(src, seg, n):
    return jax.ops.segment_sum(src, seg, n)
kernel_name = 'mk_flamingo_gated_d2_seqx_r8_aa52e5'

def setup_inputs(seed: int=0):
    np.random.seed(seed)
    _w = jnp.asarray

    def _rec_inputs():
        import jax
        import jax.numpy as jnp
        _rk = jax.random.key(seed)
        x = -0.0003929 + 0.9999 * jax.random.normal(jax.random.fold_in(_rk, 1), (32, 128, 128), jnp.float32)
        _lenS = 128 - jax.random.randint(jax.random.fold_in(_rk, 7), (32,), 0, max(1, 128 // 4) + 1, jnp.int32)
        _lenS2 = 77 - jax.random.randint(jax.random.fold_in(_rk, 8), (32,), 0, max(1, 77 // 4) + 1, jnp.int32)
        _ctx_1024P = jax.random.normal(jax.random.fold_in(_rk, 11), (32, 16, 128), jnp.float32)
        _ctx_1024c = jax.random.dirichlet(jax.random.fold_in(_rk, 511), 0.3 * jnp.ones((16,), jnp.float32), (32, 77))
        _ctx_1024t = jnp.einsum('bsk,bkd->bsd', _ctx_1024c, _ctx_1024P)
        _ctx_1024t = _ctx_1024t * jax.lax.rsqrt(jnp.mean(jnp.square(_ctx_1024t)) + 1e-12) * 0.953939
        ctx_1024 = 2.81802e-05 + 1.00001 * (_ctx_1024t + 0.3 * jax.random.normal(jax.random.fold_in(_rk, 611), (32, 77, 128), jnp.float32))
        _validS = jnp.arange(128)[None, :] < _lenS[:, None]
        _validS2 = jnp.arange(77)[None, :] < _lenS2[:, None]
        _causal = jnp.tril(jnp.ones((128, 128), dtype=bool))
        mask_BxSxS2_ik1 = jnp.where(jnp.broadcast_to(_validS2[:, None, :], (32, 128, 77)), 1, 0).astype(jnp.int32)
        mask_BxS2_bf0 = jnp.logical_not(jnp.ones((32, 77), dtype=bool))
        _g = jax.random.normal(jax.random.fold_in(_rk, 9001), (2, 2), jnp.float32)
        _g = jnp.sign(_g) * jnp.maximum(jnp.abs(_g), 1.0) + (_g == 0) * 1.0
        g_xattn = _g[0]
        g_ffn = _g[1]
        return (x, ctx_1024, mask_BxSxS2_ik1, mask_BxS2_bf0, g_xattn, g_ffn)
    x, ctx_1024, mask_BxSxS2_ik1, mask_BxS2_bf0, g_xattn, g_ffn = _rec_inputs()

    def _L0_xattn_setup():
        import jax, jax.numpy as jnp
        import numpy as np
        B, L, H = (8, 256, 128)
        SCALE = float(np.sqrt(H))
        EPS = 1e-05
        key = jax.random.key(seed)
        ks = jax.random.split(key, 12)
        s = 1.0 / np.sqrt(H)
        return {'queries': jax.random.normal(ks[0], (B, L, H), jnp.float32), 'keys': jax.random.normal(ks[1], (B, L, H), jnp.float32), 'values': jax.random.normal(ks[2], (B, L, H), jnp.float32), 'mask': jax.random.randint(ks[3], (B, L, L), 0, 2, jnp.int32), 'Wq': jax.random.normal(ks[4], (H, H), jnp.float32) * s, 'bq': jnp.zeros((H,), jnp.float32), 'Wk': jax.random.normal(ks[5], (H, H), jnp.float32) * s, 'bk': jnp.zeros((H,), jnp.float32), 'Wv': jax.random.normal(ks[6], (H, H), jnp.float32) * s, 'bv': jnp.zeros((H,), jnp.float32), 'ln_gamma': jnp.ones((H,), jnp.float32), 'ln_beta': jnp.zeros((H,), jnp.float32)}
    _L0_xattn_all = _L0_xattn_setup()
    _L0_xattn_in = {k: v for k, v in _L0_xattn_all.items() if k in ('Wq', 'bq', 'Wk', 'bk', 'Wv', 'bv', 'ln_gamma', 'ln_beta')}
    del _L0_xattn_all

    def _L0_ffn_setup():
        import jax, jax.numpy as jnp
        import numpy as np
        B, T, C, H, E = (1, 32, 128, 256, 8)
        STD = 0.02
        key = jax.random.key(seed)
        ks = jax.random.split(key, 8)
        f32 = jnp.float32
        return {'x': jax.random.normal(ks[0], (B, T, C), f32), 'up': jax.random.normal(ks[1], (E, H, C), f32) * STD, 'gate': jax.random.normal(ks[2], (E, H, C), f32) * STD, 'down': jax.random.normal(ks[3], (E, C, H), f32) * STD, 'router': jax.random.normal(ks[4], (E, C), f32) * STD, 'w_up_s': jax.random.normal(ks[5], (H, C), f32) * STD, 'w_gate_s': jax.random.normal(ks[6], (H, C), f32) * STD, 'w_down_s': jax.random.normal(ks[7], (C, H), f32) * STD}
    _L0_ffn_all = _L0_ffn_setup()
    _L0_ffn_in = {k: v for k, v in _L0_ffn_all.items() if k in ('up', 'gate', 'down', 'router', 'w_up_s', 'w_gate_s', 'w_down_s')}
    del _L0_ffn_all

    def _L1_xattn_setup():
        import jax, jax.numpy as jnp
        import numpy as np
        DIM = 128
        N_HEADS = 16
        HEAD_DIM = DIM // N_HEADS
        MAX_DIST = 128
        B, S = (2, 256)

        def _rel_bias(bias_table, q_len, k_len):
            q_pos = jnp.arange(q_len)
            k_pos = jnp.arange(k_len)
            rel = jnp.clip(k_pos[None, :] - q_pos[:, None], -MAX_DIST, MAX_DIST) + MAX_DIST
            bias = bias_table[rel]
            return jnp.transpose(bias, (2, 0, 1))
        key = jax.random.key(seed)
        ks = jax.random.split(key, 16)
        inp = {'query': jax.random.normal(ks[0], (B, S, DIM), jnp.float32), 'key': jax.random.normal(ks[1], (B, S, DIM), jnp.float32), 'value': jax.random.normal(ks[2], (B, S, DIM), jnp.float32), 'key_padding_mask': jnp.zeros((B, S), dtype=bool), 'Wq': jax.random.normal(ks[3], (DIM, DIM), jnp.float32) * DIM ** (-0.5), 'bq': jnp.zeros((DIM,), jnp.float32), 'Wk': jax.random.normal(ks[4], (DIM, DIM), jnp.float32) * DIM ** (-0.5), 'bk': jnp.zeros((DIM,), jnp.float32), 'Wv': jax.random.normal(ks[5], (DIM, DIM), jnp.float32) * DIM ** (-0.5), 'bv': jnp.zeros((DIM,), jnp.float32), 'Wo': jax.random.normal(ks[6], (DIM, DIM), jnp.float32) * DIM ** (-0.5), 'bo': jnp.zeros((DIM,), jnp.float32), 'logit_scale': jax.random.normal(ks[7], (N_HEADS,), jnp.float32) * 0.1, 'bias_table': jax.random.normal(ks[8], (2 * MAX_DIST + 1, N_HEADS), jnp.float32) * 0.02}
        return inp
    _L1_xattn_all = _L1_xattn_setup()
    _L1_xattn_in = {k: v for k, v in _L1_xattn_all.items() if k in ('Wq', 'bq', 'Wk', 'bk', 'Wv', 'bv', 'Wo', 'bo', 'logit_scale', 'bias_table')}
    del _L1_xattn_all

    def _L1_ffn_setup():
        import jax, jax.numpy as jnp
        import numpy as np
        B, S, D, T = (4, 512, 128, 8)
        key = jax.random.key(seed)
        k1, k2, k3, k4 = jax.random.split(key, 4)
        x = jax.random.normal(k1, (B, S, D), dtype=jnp.float32)
        tile_sigs = jax.random.normal(k2, (T, D), dtype=jnp.float32)
        bound = 1.0 / np.sqrt(D)
        W = jax.random.uniform(k3, (T, D, D), minval=-bound, maxval=bound, dtype=jnp.float32)
        b = jax.random.uniform(k4, (T, D), minval=-bound, maxval=bound, dtype=jnp.float32)
        return {'x': x, 'tile_sigs': tile_sigs, 'W': W, 'b': b}
    _L1_ffn_all = _L1_ffn_setup()
    _L1_ffn_in = {k: v for k, v in _L1_ffn_all.items() if k in ('tile_sigs', 'W', 'b')}
    del _L1_ffn_all
    return {'x': x, 'ctx_1024': ctx_1024, 'mask_BxSxS2_ik1': mask_BxSxS2_ik1, 'mask_BxS2_bf0': mask_BxS2_bf0, 'g_xattn': g_xattn, 'g_ffn': g_ffn, 'L0_xattn_Wq': _L0_xattn_in['Wq'], 'L0_xattn_bq': _L0_xattn_in['bq'], 'L0_xattn_Wk': _L0_xattn_in['Wk'], 'L0_xattn_bk': _L0_xattn_in['bk'], 'L0_xattn_Wv': _L0_xattn_in['Wv'], 'L0_xattn_bv': _L0_xattn_in['bv'], 'L0_xattn_ln_gamma': _L0_xattn_in['ln_gamma'], 'L0_xattn_ln_beta': _L0_xattn_in['ln_beta'], 'L0_ffn_up': _L0_ffn_in['up'], 'L0_ffn_gate': _L0_ffn_in['gate'], 'L0_ffn_down': _L0_ffn_in['down'], 'L0_ffn_router': _L0_ffn_in['router'], 'L0_ffn_w_up_s': _L0_ffn_in['w_up_s'], 'L0_ffn_w_gate_s': _L0_ffn_in['w_gate_s'], 'L0_ffn_w_down_s': _L0_ffn_in['w_down_s'], 'L1_xattn_Wq': _L1_xattn_in['Wq'], 'L1_xattn_bq': _L1_xattn_in['bq'], 'L1_xattn_Wk': _L1_xattn_in['Wk'], 'L1_xattn_bk': _L1_xattn_in['bk'], 'L1_xattn_Wv': _L1_xattn_in['Wv'], 'L1_xattn_bv': _L1_xattn_in['bv'], 'L1_xattn_Wo': _L1_xattn_in['Wo'], 'L1_xattn_bo': _L1_xattn_in['bo'], 'L1_xattn_logit_scale': _L1_xattn_in['logit_scale'], 'L1_xattn_bias_table': _L1_xattn_in['bias_table'], 'L1_ffn_tile_sigs': _L1_ffn_in['tile_sigs'], 'L1_ffn_W': _L1_ffn_in['W'], 'L1_ffn_b': _L1_ffn_in['b']}

def reference(x, ctx_1024, mask_BxSxS2_ik1, mask_BxS2_bf0, g_xattn, g_ffn, L0_xattn_Wq, L0_xattn_bq, L0_xattn_Wk, L0_xattn_bk, L0_xattn_Wv, L0_xattn_bv, L0_xattn_ln_gamma, L0_xattn_ln_beta, L0_ffn_up, L0_ffn_gate, L0_ffn_down, L0_ffn_router, L0_ffn_w_up_s, L0_ffn_w_gate_s, L0_ffn_w_down_s, L1_xattn_Wq, L1_xattn_bq, L1_xattn_Wk, L1_xattn_bk, L1_xattn_Wv, L1_xattn_bv, L1_xattn_Wo, L1_xattn_bo, L1_xattn_logit_scale, L1_xattn_bias_table, L1_ffn_tile_sigs, L1_ffn_W, L1_ffn_b):
    import jax
    import jax.numpy as jnp

    def _L0_xattn_ref(queries, keys, values, mask, Wq, bq, Wk, bk, Wv, bv, ln_gamma, ln_beta):
        import jax, jax.numpy as jnp
        import numpy as np
        B, L, H = (8, 256, 128)
        SCALE = float(np.sqrt(H))
        EPS = 1e-05
        Q = queries @ Wq + bq
        K = keys @ Wk + bk
        V = values @ Wv + bv
        scores = jnp.einsum('bik,bjk->bij', Q, K) / SCALE
        scores = jnp.where(mask == 0, -jnp.inf, scores)
        probs = jax.nn.softmax(scores, axis=-1)
        context = jnp.einsum('bij,bjk->bik', probs, V)
        mu = jnp.mean(context, axis=-1, keepdims=True)
        var = jnp.var(context, axis=-1, keepdims=True)
        normed = (context - mu) * jax.lax.rsqrt(var + EPS)
        return normed * ln_gamma + ln_beta

    def _L0_ffn_ref(x, up, gate, down, router, w_up_s, w_gate_s, w_down_s):
        import jax, jax.numpy as jnp
        import numpy as np
        B, T, C, H, E = (1, 32, 128, 256, 8)
        STD = 0.02
        b, t, c = x.shape
        x_ = x.reshape(b * t, c)
        logits = x_ @ router.T
        idx = jnp.argmax(logits, axis=-1)
        onehot = jax.nn.one_hot(idx, router.shape[0], dtype=x.dtype)
        u = jnp.einsum('bc,ehc->ebh', x_, up)
        g = jnp.einsum('bc,ehc->ebh', x_, gate)
        h = jax.nn.silu(g) * u
        ye = jnp.einsum('ebh,ech->ebc', h, down)
        y = jnp.einsum('ebc,be->bc', ye, onehot)
        ys = jax.nn.silu(x_ @ w_gate_s.T) * (x_ @ w_up_s.T) @ w_down_s.T
        return (y + ys).reshape(b, t, c)

    def _L1_xattn_ref(query, key, value, key_padding_mask, Wq, bq, Wk, bk, Wv, bv, Wo, bo, logit_scale, bias_table):
        import jax, jax.numpy as jnp
        import numpy as np
        DIM = 128
        N_HEADS = 16
        HEAD_DIM = DIM // N_HEADS
        MAX_DIST = 128
        B, S = (2, 256)

        def _rel_bias(bias_table, q_len, k_len):
            q_pos = jnp.arange(q_len)
            k_pos = jnp.arange(k_len)
            rel = jnp.clip(k_pos[None, :] - q_pos[:, None], -MAX_DIST, MAX_DIST) + MAX_DIST
            bias = bias_table[rel]
            return jnp.transpose(bias, (2, 0, 1))
        b, tq, _ = query.shape
        tk = key.shape[1]

        def proj(x, W, bias):
            y = x @ W + bias
            return y.reshape(b, -1, N_HEADS, HEAD_DIM).transpose(0, 2, 1, 3)
        q = proj(query, Wq, bq)
        k = proj(key, Wk, bk)
        v = proj(value, Wv, bv)
        base_scale = HEAD_DIM ** (-0.5)
        scale = base_scale * jnp.minimum(jnp.exp(logit_scale), 4.0)
        scores = jnp.einsum('bhqd,bhkd->bhqk', q, k) * scale[None, :, None, None]
        scores = scores + _rel_bias(bias_table, tq, tk)[None]
        neg = -jnp.finfo(scores.dtype).max
        scores = jnp.where(key_padding_mask[:, None, None, :], neg, scores)
        attn = jax.nn.softmax(scores, axis=-1)
        out = jnp.einsum('bhqk,bhkd->bhqd', attn, v)
        out = out.transpose(0, 2, 1, 3).reshape(b, tq, DIM)
        out = out @ Wo + bo
        return out

    def _L1_ffn_ref(x, tile_sigs, W, b):
        import jax, jax.numpy as jnp
        import numpy as np
        B, S, D, T = (4, 512, 128, 8)
        scores = jnp.einsum('bsd,td->bst', x, jnp.sign(tile_sigs))
        idx = jnp.argmax(scores, axis=-1)
        all_out = jnp.einsum('bsd,tde->bste', x, W) + b[None, None]
        out = jnp.take_along_axis(all_out, idx[:, :, None, None], axis=2)
        return out[:, :, 0, :]
    x = x + jnp.tanh(g_xattn[0]) * _L0_xattn_ref(_layernorm(x, axis=-1), ctx_1024, ctx_1024, mask_BxSxS2_ik1, L0_xattn_Wq, L0_xattn_bq, L0_xattn_Wk, L0_xattn_bk, L0_xattn_Wv, L0_xattn_bv, L0_xattn_ln_gamma, L0_xattn_ln_beta)
    x = x + jnp.tanh(g_ffn[0]) * _L0_ffn_ref(_layernorm(x, axis=-1), L0_ffn_up, L0_ffn_gate, L0_ffn_down, L0_ffn_router, L0_ffn_w_up_s, L0_ffn_w_gate_s, L0_ffn_w_down_s)
    x = x + jnp.tanh(g_xattn[1]) * _L1_xattn_ref(_layernorm(x, axis=-1), ctx_1024, ctx_1024, mask_BxS2_bf0, L1_xattn_Wq, L1_xattn_bq, L1_xattn_Wk, L1_xattn_bk, L1_xattn_Wv, L1_xattn_bv, L1_xattn_Wo, L1_xattn_bo, L1_xattn_logit_scale, L1_xattn_bias_table)
    x = x + jnp.tanh(g_ffn[1]) * _L1_ffn_ref(_layernorm(x, axis=-1), L1_ffn_tile_sigs, L1_ffn_W, L1_ffn_b)
    return x

_drawn_inputs = setup_inputs


def setup_inputs(seed=0):
    import zlib

    import numpy as np

    out = dict(_drawn_inputs(seed))
    spreads = {'g_ffn': (-1.0, 0.6),
     'L0_xattn_bq': (0.0, 0.1),
     'L0_xattn_bk': (0.0, 0.8),
     'L0_xattn_bv': (0.0, 0.1),
     'L0_xattn_ln_gamma': (1.0, 0.2),
     'L0_xattn_ln_beta': (0.0, 0.1),
     'L1_xattn_bq': (0.0, 0.1),
     'L1_xattn_bk': (0.0, 0.8),
     'L1_xattn_bv': (0.0, 0.1),
     'L1_xattn_bo': (0.0, 0.1)}
    factors = {'L0_ffn_router': 2.802, 'L1_xattn_bias_table': 3.398}
    for name, (base, spread) in spreads.items():
        noise = np.random.default_rng([zlib.crc32(name.encode()), seed]).standard_normal(out[name].shape)
        drawn = base * np.exp(spread * noise) if base else spread * noise
        out[name] = jnp.asarray(drawn.astype(out[name].dtype))
    for name, factor in factors.items():
        out[name] = (out[name] * factor).astype(out[name].dtype)
    return out
```

```python
from contextlib import ExitStack

import concourse.bass as bass
import numpy as np
from concourse import mybir

F32 = mybir.dt.float32
BF16 = mybir.dt.bfloat16
I32 = mybir.dt.int32
U32 = mybir.dt.uint32
U8 = mybir.dt.uint8
ALU = mybir.AluOpType
ACT = mybir.ActivationFunctionType
AX = mybir.AxisListType

B, S, D = 32, 128, 128
SK = 77
E, H = 8, 256
HC = H // 128
NH, HD = 16, 8
HG = 4
NCH = NH // HG
T = 8
NTILE = 40
SLOTS = NTILE * 128
PAIR = 2
NG = B // PAIR
EPS = 1e-5
NEG = -3.0e38
PADDED = -(2.0 ** 100)

C_IDENT = 0
C_TRI = C_IDENT + 128
C_HEAD = C_TRI + 128
C_RANK = C_HEAD + NH
C_SEG = C_RANK + E
C_TILE = C_SEG + E * B
C_SEL = C_TILE + NTILE
C_END = C_SEL + NH * SK


def constants():
    c = np.zeros((128, C_END), np.float32)
    p = np.arange(128)
    c[:, C_IDENT:C_TRI] = np.eye(128)
    c[:, C_TRI:C_HEAD] = p[:, None] < p[None, :]
    c[:, C_HEAD:C_RANK] = p[:, None] // HD == np.arange(NH)[None, :]
    c[:, C_RANK:C_SEG] = E - np.arange(E)
    c[:, C_SEG:C_TILE] = np.arange(E * B) % B != 0
    c[:, C_TILE:C_SEL] = 128 * np.arange(NTILE)
    sel = (np.arange(NH)[:, None] == np.arange(NH)[None, :]).astype(np.float32)
    c[:NH, C_SEL:C_END] = np.repeat(sel, SK, axis=1)
    return c


def wait(eng, sem, value):
    if isinstance(value, int) and value <= 0:
        return
    eng.wait_ge(sem, value)


def apart(eng, started):
    eng.wait_ge(started, 1)


def pipeline(eng, n, stages):
    first = min(lag for _, lag in stages)
    stages = [(stage, lag - first) for stage, lag in stages]
    head = (max(lag for _, lag in stages) + 1) // 2 + 1

    def turn(i):
        for u in range(2):
            for stage, lag in stages:
                item = 2 * i + u - lag
                if isinstance(item, int) and not 0 <= item < n:
                    continue
                stage(item, (u - lag) % 2)

    for i in range(head):
        turn(i)
    with eng.Fori(head, n // 2) as i:
        turn(i)
    for i in range(n // 2, n // 2 + head - 1):
        turn(i)


def landed(eng, sems, item, parity):
    eng.wait_ge(sems[parity], 8 * (item - parity) + 16)


def phase(f):
    def run(nc, *rest):
        with ExitStack() as own:
            def sb(name, shape, dt=F32):
                return own.enter_context(nc.sbuf_tensor(name, shape, dt))
            f(nc, sb, *rest)
    return run


def build(nc, a, out):
    with ExitStack() as ctx:
        def sb(name, shape, dt=F32):
            return ctx.enter_context(nc.sbuf_tensor(name, shape, dt))

        def sem(name):
            return ctx.enter_context(nc.semaphore(name))

        def sems(stem, names):
            return {n: sem(f"{stem}_{n}") for n in names.split()}

        bank = [ctx.enter_context(nc.psum_tensor(f"bank{i}", [128, 512], F32)) for i in range(8)]

        sorted_x = nc.dram_tensor("sorted_x", (SLOTS, D), F32).ap()
        sorted_y = nc.dram_tensor("sorted_y", (SLOTS, D), F32).ap()

        wide_kq = nc.dram_tensor("wide_kq", (NH, SK, S), F32).ap()
        wide_qk = nc.dram_tensor("wide_qk", (NH, S, SK), F32).ap()

        X = sb("X", [128, B, D])
        XN = sb("XN", [128, B, D])
        XNT = sb("XNT", [128, B, S])
        K1T = sb("K1T", [128, B, SK])
        V1 = sb("V1", [SK, B, D])
        LG = sb("LG", [128, B, E])
        stats0 = sb("stats0", [128, B, 6])
        mean0 = sb("mean0", [128, B])
        var0 = sb("var0", [128, B])
        rstd0 = sb("rstd0", [128, B])

        cst = sb("cst", [128, C_END])
        ident = cst[:, C_IDENT:C_TRI]
        tri = cst[:, C_TRI:C_HEAD]
        headmask = cst[:, C_HEAD:C_RANK]
        rankrow = cst[:, C_RANK:C_SEG]
        segments = cst[:, C_SEG:C_TILE]
        tilestart = cst[0:1, C_TILE:C_SEL]
        identb = sb("identb", [128, 128], BF16)
        selb = sb("selb", [NH, NH, SK], BF16)
        ones = sb("ones", [128, 128])
        onesb = sb("onesb", [1, 128], BF16)
        zeros = sb("zeros", [128, 512])
        power = sb("power", [128, B])
        eps = sb("eps", [128, 1])
        gates = sb("gates", [128, 4])
        tg = sb("tg", [128, 4])
        wqT = sb("wqT", [128, D])
        wkT = sb("wkT", [128, D])
        wqk = sb("wqk", [128, D])
        cols = sb("cols", [128, 8])
        m0 = sb("m0", [128, 1])
        uq = sb("uq", [128, 1])
        c0 = sb("c0", [1, 1])
        wv01 = sb("wv01", [128, 2 * D])
        bv01 = sb("bv01", [SK, 2 * D])
        gain = sb("gain", [128, D])
        shift = sb("shift", [128, D])
        wk1 = sb("wk1", [128, D])
        wq1 = sb("wq1", [128, D])
        wo1 = sb("wo1", [128, D])
        bo1 = sb("bo1", [128, D])
        router = sb("router", [128, E])
        qscale = sb("qscale", [128, 1])
        qbias = sb("qbias", [128, 1])
        wgs = sb("wgs", [128, H])
        wus = sb("wus", [128, H])
        wds = sb("wds", [128, HC, D])
        wgu = sb("wgu", [128, E, 2 * H])
        wdn = sb("wdn", [128, E, HC, D])
        sgn = sb("sgn", [128, T])
        w2 = sb("w2", [128, T, D])
        b2 = sb("b2", [T, D])
        biasT = sb("biasT", [SK, NH, S])
        biasQ = sb("biasQ", [128, NH, SK], BF16)
        padT = sb("padT", [SK, B])
        padR = sb("padR", [1, B, SK], BF16)
        nmax = sb("nmax", [128, B])
        slot = sb("slot", [128, B], U32)
        tile_expert = sb("tile_expert", [1, NTILE], I32)

        s_w = sem("s_w")
        s_x = sem("s_x")
        s_zero = sem("s_zero")
        s_set = sem("s_set")
        s_const = sem("s_const")
        s_pe0 = sem("s_pe0")
        s_act0 = sem("s_act0")
        s_dve0 = sem("s_dve0")
        s_pool0 = sem("s_pool0")
        s_stat = sem("s_stat")
        s_bias = sem("s_bias")
        s_window = sem("s_window")
        biasQf = XNT[:, 0:10, :].rearrange("p b s -> p (b s)")[:, 0:NH * SK]

        padTi = XNT[0:SK, 10, 0:B // 4].bitcast(U8)
        padRi = XNT[0:1, 11:11 + 5, :].rearrange("p b s -> p (b s)")[:, 0:B * SK // 4].bitcast(U8)

        row = lambda v: v.rearrange("(o n) -> o n", o=1)
        column = lambda v: v.rearrange("(n o) -> n o", o=1)

        loads = [
            (wqT[:, :], a["wqT0"]), (wkT[:, :], a["wkT0"]),
            (cols[:, 0:1], column(a["bq0"])), (cols[:, 1:2], column(a["bk0"])),
            (cols[:, 2:3], column(a["bq1"])), (cols[:, 3:4], column(a["bk1"])),
            (cols[:, 4:5], column(a["logit_scale"])),
            (wv01[:, 0:D], a["wv0"]), (wv01[:, D:2 * D], a["wv1"]),
            (bv01[:, 0:D], row(a["bv0"]).to_broadcast([SK, D])),
            (bv01[:, D:2 * D], row(a["bv1"]).to_broadcast([SK, D])),
            (gain[:, :], row(a["gamma"]).to_broadcast([128, D])),
            (shift[:, :], row(a["beta"]).to_broadcast([128, D])),
            (bo1[:, :], row(a["bo1"]).to_broadcast([128, D])),
            (gates[:, 0:2], row(a["g_xattn"]).to_broadcast([128, 2])),
            (gates[:, 2:4], row(a["g_ffn"]).to_broadcast([128, 2])),
            (wk1[:, :], a["wk1"]), (wq1[:, :], a["wq1"]), (wo1[:, :], a["wo1"]),
            (router[:, :], a["router"]), (wgs[:, :], a["wgs"]), (wus[:, :], a["wus"]),
            (wds[:, :, :], a["wds"]), (wgu[:, :, :], a["wgu"]), (wdn[:, :, :, :], a["wdn"]),
            (padTi, a["padT"]), (padRi, row(a["pad"])),
            (sgn[:, :], a["sigs"]), (w2[:, :, :], a["w2"]), (b2[:, :], a["b2"]),
        ]
        n_loads = len(loads)
        table = a["table"].tensor
        width = a["table"].shape[1]

        with nc.Block() as block:
            @block.sync
            def _(sp):
                sp.dma_start(cst[:, :], a["cst"]).then_inc(s_const, 16)
                for q in range(4):
                    sp.dma_start(X[:, 8 * q:8 * q + 8, :],
                                 a["x"][8 * q:8 * q + 8].rearrange("b s d -> s b d")).then_inc(s_x, 16)
                for dst, src in loads[1::2]:
                    sp.dma_start(dst, src).then_inc(s_w, 16)
                sp.dma_start(wide_kq, bass.AP(
                    tensor=a["table_rev"].tensor, offset=width - 1 - 128,
                    ap=[[width, NH], [-1, SK], [1, S]])).then_inc(s_window, 16)
                sp.dma_start(wide_qk, bass.AP(
                    tensor=table, offset=128, ap=[[width, NH], [-1, 128], [1, SK]])).then_inc(s_window, 16)
                sp.wait_ge(s_window, 32)
                sp.dma_start(biasT[:, :, :], wide_kq.rearrange("h k q -> k h q")).then_inc(s_bias, 16)
                sp.dma_start(biasQf.rearrange("p (h k) -> p h k", h=NH),
                             wide_qk.rearrange("h q k -> q h k")).then_inc(s_bias, 16)
                sp.wait_ge(s_set, 1)
                for q in range(SLOTS // 512):
                    sp.dma_start(sorted_x[512 * q:512 * q + 512].rearrange("(p r) d -> p (r d)", p=128),
                                 zeros[:, :]).then_inc(s_zero, 16)
                sp.wait_ge(s_zero, 16 * (SLOTS // 512))

            @block.gpsimd
            def _(pool):
                pool.wait_ge(s_stat, B + 6)
                nc.gpsimd.tensor_tensor(rstd0[:, :], var0[:, :], power[:, :], ALU.pow).then_inc(s_pool0, 1)

            @block.scalar
            def _(act):
                for dst, src in loads[0::2]:
                    act.dma_start(dst, src).then_inc(s_w, 16)
                act.wait_ge(s_w, 16 * n_loads)
                nc.scalar.activation(tg[:, :], gates[:, :], ACT.Tanh).then_inc(s_act0, 1)
                nc.scalar.activation(qscale[:, :], cols[:, 4:5], ACT.Exp).then_inc(s_act0, 1)
                nc.scalar.activation(sgn[:, :], sgn[:, :], ACT.Sign).then_inc(s_act0, 1)
                act.wait_ge(s_pe0, 1)
                nc.scalar.activation(wqk[:, :], bank[0][:, 0:D], ACT.Copy).then_inc(s_act0, 1)
                nc.scalar.activation(m0[:, :], bank[0][:, D:D + 1], ACT.Copy, scale=D ** -0.5).then_inc(s_act0, 1)
                nc.scalar.activation(uq[:, :], bank[0][:, D + 1:D + 2], ACT.Copy).then_inc(s_act0, 1)
                nc.scalar.activation(c0[:, :], bank[0][0:1, D + 2:D + 3], ACT.Copy, scale=D ** -0.5).then_inc(s_act0, 1)

            @block.tensor
            def _(pe):
                pe.wait_ge(s_w, 16 * n_loads)
                nc.tensor.matmul(bank[0][:, 0:D], wkT[:, :], wqT[:, :], start=True, stop=True)
                nc.tensor.matmul(bank[0][:, D:D + 1], wqT[:, :], cols[:, 1:2], start=True, stop=True)
                nc.tensor.matmul(bank[0][:, D + 1:D + 2], wkT[:, :], cols[:, 0:1], start=True, stop=True)
                nc.tensor.matmul(bank[0][0:1, D + 2:D + 3], cols[:, 0:1], cols[:, 1:2],
                                 start=True, stop=True).then_inc(s_pe0, 1)

            @block.vector
            def _(dve):
                nc.vector.memset(zeros[:, :], 0.0).then_inc(s_set, 1)
                nc.vector.memset(ones[:, :], 1.0).then_inc(s_set, 1)
                nc.vector.memset(onesb[:, :], 1.0).then_inc(s_set, 1)
                nc.vector.memset(power[:, :], -0.5).then_inc(s_set, 1)
                nc.vector.memset(eps[:, :], EPS)
                dve.wait_ge(s_const, 16)
                nc.vector.tensor_copy(identb[:, :], ident)
                nc.vector.tensor_copy(selb[:, :, :].rearrange("r h k -> r (h k)"), cst[0:NH, C_SEL:C_END])
                dve.wait_ge(s_x, 64)
                with dve.Fori(0, B) as b:
                    nc.vector.bn_stats(stats0[:, b, :], X[:, b, :]).then_inc(s_stat, 1)
                dve.wait_ge(s_stat, B)
                me, mo = stats0[:, :, 1], stats0[:, :, 4]
                half = mean0[:, :]
                nc.vector.tensor_tensor(var0[:, :], me, mo, ALU.subtract).then_inc(s_stat, 1)
                dve.wait_ge(s_stat, B + 1)
                nc.vector.scalar_tensor_tensor(out=var0[:, :], in0=var0[:, :], scalar=D / 4.0, in1=var0[:, :],
                                               op0=ALU.mult, op1=ALU.mult).then_inc(s_stat, 1)
                nc.vector.tensor_tensor(half, stats0[:, :, 2], stats0[:, :, 5], ALU.add).then_inc(s_stat, 1)
                dve.wait_ge(s_stat, B + 3)
                nc.vector.tensor_tensor(var0[:, :], var0[:, :], half, ALU.add).then_inc(s_stat, 1)
                dve.wait_ge(s_stat, B + 4)
                nc.vector.tensor_scalar(var0[:, :], var0[:, :], 1.0 / D, EPS, ALU.mult, ALU.add).then_inc(s_stat, 1)
                nc.vector.tensor_tensor(half, me, mo, ALU.add).then_inc(s_stat, 1)
                dve.wait_ge(s_stat, B + 6)
                nc.vector.tensor_scalar(mean0[:, :], mean0[:, :], 0.5, None, ALU.mult).then_inc(s_dve0, 1)
                dve.wait_ge(s_w, 16 * n_loads)
                dve.wait_ge(s_act0, 2)
                scaled = [(gain, 0), (shift, 0), (wo1, 1), (bo1, 1)]
                for t, g in scaled:
                    nc.vector.tensor_scalar(t[:, :], t[:, :], tg[:, g:g + 1], None, ALU.mult)
                nc.vector.tensor_scalar(wds[:, :, :], wds[:, :, :], tg[:, 2:3], None, ALU.mult)
                nc.vector.tensor_scalar(wdn[:, :, :, :], wdn[:, :, :, :], tg[:, 2:3], None, ALU.mult)
                nc.vector.tensor_scalar(w2[:, :, :], w2[:, :, :], tg[:, 3:4], None, ALU.mult)
                nc.vector.tensor_scalar(b2[:, :], b2[:, :], tg[0:T, 3:4], None, ALU.mult)
                nc.vector.tensor_scalar(padT[:, :], padTi, PADDED, None, ALU.mult)
                nc.vector.tensor_scalar(padR[:, :, :].rearrange("p b k -> p (b k)"), padRi, PADDED, None, ALU.mult)
                nc.vector.tensor_scalar(qscale[:, :], qscale[:, :], 4.0, HD ** -0.5, ALU.min, ALU.mult).then_inc(s_dve0, 1)
                dve.wait_ge(s_dve0, 2)
                nc.vector.tensor_tensor(qbias[:, :], cols[:, 2:3], qscale[:, :], ALU.mult)
                dve.wait_ge(s_bias, 32)
                nc.vector.tensor_copy(biasQ[:, :, :].rearrange("p h k -> p (h k)"), biasQf).then_inc(s_dve0, 1)

        attend_0(nc, sem, sems, bank, a, locals())
        route(nc, sem, sems, bank, locals())
        experts(nc, sem, sems, bank, locals())
        collect(nc, sem, sems, bank, locals())
        attend_1(nc, sem, sems, bank, out, locals())


@phase
def attend_0(nc, sb, sem, sems, bank, a, m):
    X, XN, XNT, K1T, V1, LG = (m[k] for k in ("X", "XN", "XNT", "K1T", "V1", "LG"))
    mean0, rstd0, power, ident, ones = (m[k] for k in ("mean0", "rstd0", "power", "ident", "ones"))
    wqk, m0, uq, c0, wk1, cols = (m[k] for k in ("wqk", "m0", "uq", "c0", "wk1", "cols"))
    wv01, bv01, gain, shift, router = (m[k] for k in ("wv01", "bv01", "gain", "shift", "router"))
    started, eps, nmax = m["s_set"], m["eps"], m["nmax"]
    two = range(2)
    PK = PAIR * SK
    ctxT = [sb(f"ctxT{u}", [128, PK]) for u in two]
    mask = [sb(f"mask{u}", [128, PAIR, SK], I32) for u in two]
    mbias = [sb(f"mbias{u}", [128, PAIR, SK]) for u in two]
    M = [sb(f"M{u}", [128, PK]) for u in two]
    crow = [sb(f"crow{u}", [1, PK]) for u in two]
    V0 = [sb(f"V0{u}", [SK, PAIR, D + 1]) for u in two]
    xn = [sb(f"xn{u}", [128, PAIR, D]) for u in two]
    xnT = [sb(f"xnT{u}", [128, PAIR, S]) for u in two]
    sm = [sb(f"sm{u}", [128, PAIR, SK]) for u in two]
    P = [sb(f"P{u}", [128, PAIR, SK]) for u in two]
    PT = [sb(f"PT{u}", [SK, PAIR, S]) for u in two]
    st = [sb(f"st{u}", [128, PAIR, 6]) for u in two]
    mv = [sb(f"mv{u}", [128, PAIR, 2]) for u in two]
    es = [sb(f"es{u}", [128, PAIR]) for u in two]
    vr = [sb(f"vr{u}", [128, PAIR]) for u in two]
    ru = [sb(f"ru{u}", [128, PAIR]) for u in two]
    t1 = [sb(f"t1{u}", [128, PAIR, D]) for u in two]
    xb = [sb(f"xb{u}", [128, PAIR, D]) for u in two]
    st1 = [sb(f"st1{u}", [128, PAIR, 6]) for u in two]
    mv1 = [sb(f"mv1{u}", [128, PAIR, 2]) for u in two]
    r1 = [sb(f"r1{u}", [128, PAIR]) for u in two]
    v1e = [sb(f"v1e{u}", [128, PAIR]) for u in two]
    xn1 = [sb(f"xn1{u}", [128, PAIR, D]) for u in two]
    xn1T = [sb(f"xn1T{u}", [128, PAIR, S]) for u in two]

    bXT, bS, bPT, bU, bV, bMK, bT2, bLG = bank
    U = bU[:, 0:PAIR * (D + 1)].rearrange("p (b d) -> p b d", b=PAIR)
    s = sems("a", "set kv_v kv_m vev mev mb xn xT xnT sc sm mx ex pT pTs u ust umv ves vru t1 xb x1 "
                  "xst xmv vx r1 xn1 xn1c xT2 xT2s lg lgs uvr")
    l_ctx = [sem(f"a_ctx{u}") for u in two]
    l_mask = [sem(f"a_mask{u}") for u in two]

    with nc.Block() as block:
        @block.sync
        def _(sp):
            def load(g, u):
                wait(sp, s["kv_m"], g - 1)
                sp.dma_start(ctxT[u][:, :], a["ctxT"][:, bass.ds(g, 1), :].rearrange("p g k -> p (g k)")).then_inc(l_ctx[u], 16)
                wait(sp, s["mb"], g - 1)
                sp.dma_start(mask[u][:, :, :], a["mask"][:, bass.ds(PAIR * g, PAIR), :]).then_inc(l_mask[u], 16)

            pipeline(sp, NG, [(load, 0)])

        @block.tensor
        def _(pe):
            def norm_T(g, u):
                pe.wait_ge(s["xn"], g + 1)
                wait(pe, s["xnT"], g)
                for b in range(PAIR):
                    last = nc.tensor.transpose(bXT[:, b * 128:b * 128 + 128], xn[u][:, b, :], ident)
                last.then_inc(s["xT"], 1)

            def project(g, u):
                landed(pe, l_ctx, g, u)
                if isinstance(g, int) and g == 0:
                    pe.wait_ge(s["set"], 1)
                wait(pe, s["vev"], g)
                for b in range(PAIR):
                    last = nc.tensor.matmul(bV[0:SK, b * 2 * D:(b + 1) * 2 * D], ctxT[u][:, b * SK:(b + 1) * SK],
                                            wv01[:, :], start=True, stop=True)
                last.then_inc(s["kv_v"], 1)
                wait(pe, s["mev"], g)
                nc.tensor.matmul(bMK[:, 0:PK], wqk[:, :], ctxT[u][:, :], start=True, stop=True)
                nc.tensor.matmul(bMK[:, PK:2 * PK], wk1[:, :], ctxT[u][:, :], start=True, stop=True)
                nc.tensor.matmul(bMK[0:1, 2 * PK:3 * PK], uq[:, :], ctxT[u][:, :],
                                 start=True, stop=True).then_inc(s["kv_m"], 1)

            def scores(g, u):
                pe.wait_ge(s["xnT"], g + 1)
                pe.wait_ge(s["mev"], g + 1)
                wait(pe, s["sm"], g)
                for b in range(PAIR):
                    o = bS[:, b * SK:(b + 1) * SK]
                    nc.tensor.matmul(o, xnT[u][:, b, :], M[u][:, b * SK:(b + 1) * SK], start=True, stop=False)
                    last = nc.tensor.matmul(o, ones[0:1, :], crow[u][:, b * SK:(b + 1) * SK], start=False, stop=True)
                last.then_inc(s["sc"], 1)

            def probs_T(g, u):
                pe.wait_ge(s["ex"], g + 1)
                wait(pe, s["pTs"], g)
                for b in range(PAIR):
                    last = nc.tensor.transpose(bPT[0:SK, b * 128:b * 128 + 128], P[u][:, b, :], ident)
                last.then_inc(s["pT"], 1)

            def weigh(g, u):
                pe.wait_ge(s["pTs"], g + 1)
                pe.wait_ge(s["vev"], g + 1)
                wait(pe, s["t1"], g)
                for b in range(PAIR):
                    last = nc.tensor.matmul(U[:, b, :], PT[u][:, b, :], V0[u][:, b, :], start=True, stop=True)
                last.then_inc(s["u"], 1)

            def norm1_T(g, u):
                pe.wait_ge(s["xn1"], g + 1)
                wait(pe, s["xT2s"], g)
                for b in range(PAIR):
                    last = nc.tensor.transpose(bT2[:, b * 128:b * 128 + 128], xn1[u][:, b, :], ident)
                last.then_inc(s["xT2"], 1)

            def logits(g, u):
                pe.wait_ge(s["xT2s"], g + 1)
                wait(pe, s["lgs"], g)
                for b in range(PAIR):
                    last = nc.tensor.matmul(bLG[:, b * E:b * E + E], xn1T[u][:, b, :], router[:, :], start=True, stop=True)
                last.then_inc(s["lg"], 1)

            pipeline(pe, NG, [(norm_T, 0), (probs_T, 1), (project, 0), (norm1_T, 3), (weigh, 1), (scores, 0), (logits, 3)])

        @block.scalar
        def _(act):

            def exps(g, u):
                act.wait_ge(s["mx"], g + 1)
                wait(act, s["pT"], g - 1)
                for b in range(PAIR):
                    last = nc.scalar.activation(P[u][:, b, :], sm[u][:, b, :], ACT.Exp, bias=nmax[:, bass.ds(PAIR * g + b, 1)])
                last.then_inc(s["ex"], 1)

            def norm_T(g, u):
                act.wait_ge(s["xT"], g + 1)
                wait(act, s["sc"], g - 1)
                nc.scalar.activation(xnT[u][:, :, :].rearrange("p b s -> p (b s)"), bXT[:, 0:PAIR * S],
                                     ACT.Copy).then_inc(s["xnT"], 1)

            def probs_T(g, u):
                act.wait_ge(s["pT"], g + 1)
                wait(act, s["u"], g - 1)
                nc.scalar.activation(PT[u][:, :, :].rearrange("p b s -> p (b s)"), bPT[0:SK, 0:PAIR * S],
                                     ACT.Copy).then_inc(s["pTs"], 1)

            def keys(g, u):
                act.wait_ge(s["kv_m"], g + 1)
                wait(act, s["sc"], g - 1)
                nc.scalar.activation(M[u][:, :], bMK[:, 0:PK], ACT.Identity, bias=m0[:, 0:1], scale=D ** -0.5)
                nc.scalar.activation(K1T[:, bass.ds(PAIR * g, PAIR), :], bMK[:, PK:2 * PK].rearrange("p (b k) -> p b k", b=PAIR),
                                     ACT.Identity, bias=cols[:, 3:4])
                nc.scalar.activation(crow[u][:, :], bMK[0:1, 2 * PK:3 * PK], ACT.Identity, bias=c0[:, 0:1],
                                     scale=D ** -0.5).then_inc(s["mev"], 1)

            def norm1_T(g, u):
                act.wait_ge(s["xT2"], g + 1)
                wait(act, s["lg"], g - 1)
                src = bT2[:, 0:PAIR * S].rearrange("p (b s) -> p b s", b=PAIR)
                nc.scalar.activation(XNT[:, bass.ds(PAIR * g, PAIR), :], src, ACT.Copy)
                nc.scalar.activation(xn1T[u][:, :, :], src, ACT.Copy).then_inc(s["xT2s"], 1)

            def logits(g, u):
                act.wait_ge(s["lg"], g + 1)
                nc.scalar.activation(LG[:, bass.ds(PAIR * g, PAIR), :], bLG[:, 0:PAIR * E].rearrange("p (b e) -> p b e", b=PAIR),
                                     ACT.Copy).then_inc(s["lgs"], 1)

            pipeline(act, NG, [(exps, 1), (norm_T, 0), (probs_T, 1), (keys, 0), (norm1_T, 3), (logits, 3)])

        @block.vector
        def _(dve):
            for u in two:
                last = nc.vector.memset(V0[u][:, :, D:D + 1], 1.0)
            last.then_inc(s["set"], 1)

            def mask_bias(g, u):
                landed(dve, l_mask, g, u)
                wait(dve, s["sm"], g - 1)
                nc.vector.tensor_scalar(mbias[u][:, :, :], mask[u][:, :, :], 0.0, NEG, ALU.is_equal,
                                        ALU.mult).then_inc(s["mb"], 1)

            def masked(g, u):
                dve.wait_ge(s["sc"], g + 1)
                dve.wait_ge(s["mb"], g + 1)
                wait(dve, s["ex"], g - 1)
                flat = lambda t: t.rearrange("p b k -> p (b k)")
                nc.vector.tensor_tensor(flat(sm[u][:, :, :]), flat(mbias[u][:, :, :]), bS[:, 0:PK], ALU.add).then_inc(s["sm"], 1)
                dve.wait_ge(s["sm"], g + 1)
                nc.vector.tensor_reduce(nmax[:, bass.ds(PAIR * g, PAIR)], sm[u][:, :, :], AX.X, ALU.max, negate=True).then_inc(s["mx"], 1)

            def norm(g, u):
                wait(dve, s["xT"], g - 1)
                for b in range(PAIR):
                    i = PAIR * g + b
                    last = nc.vector.tensor_scalar(xn[u][:, b, :], X[:, bass.ds(i, 1), :], mean0[:, bass.ds(i, 1)],
                                                   rstd0[:, bass.ds(i, 1)], ALU.subtract, ALU.mult)
                last.then_inc(s["xn"], 1)

            def values(g, u):
                dve.wait_ge(s["kv_v"], g + 1)
                wait(dve, s["u"], g - 1)
                src = bV[0:SK, :].rearrange("p (b l d) -> p b l d", b=PAIR, l=2)
                bv = bv01[:, :].rearrange("p (l d) -> p l d", l=2)
                for layer, dst in ((0, V0[u][:, :, 0:D]), (1, V1[:, bass.ds(PAIR * g, PAIR), :])):
                    last = nc.vector.tensor_tensor(dst, src[:, :, layer, :],
                                                   bv[:, layer:layer + 1, :].to_broadcast([SK, PAIR, D]), ALU.add)
                last.then_inc(s["vev"], 1)

            def attend_stats(g, u):
                dve.wait_ge(s["u"], g + 1)
                wait(dve, s["vru"], g - 1)
                wait(dve, s["x1"], g - 1)
                for b in range(PAIR):
                    last = nc.vector.bn_stats(st[u][:, b, :], U[:, b, 0:D])
                last.then_inc(s["ust"], 1)
                nc.vector.tensor_scalar(es[u][:, :], U[:, :, D], EPS ** 0.5, None, ALU.mult)
                apart(dve, started)
                dve.wait_ge(s["ust"], g + 1)
                for b in range(PAIR):
                    last = nc.vector.bn_aggr(mv[u][:, b, :], st[u][:, b, :])
                last.then_inc(s["umv"], 1)
                dve.wait_ge(s["umv"], g + 1)
                for b in range(PAIR):
                    last = nc.vector.scalar_tensor_tensor(out=t1[u][:, b, :], in0=U[:, b, 0:D], scalar=mv[u][:, b, 0:1],
                                                          in1=gain[:, :], op0=ALU.subtract, op1=ALU.mult)
                last.then_inc(s["t1"], 1)

            def residual(g, u):
                dve.wait_ge(s["vru"], g + 1)
                dve.wait_ge(s["xb"], g + 1)
                dve.wait_ge(s["t1"], g + 1)
                wait(dve, s["r1"], g - 1)
                for b in range(PAIR):
                    last = nc.vector.scalar_tensor_tensor(out=X[:, bass.ds(PAIR * g + b, 1), :], in0=t1[u][:, b:b + 1, :],
                                                          scalar=ru[u][:, b:b + 1], in1=xb[u][:, b:b + 1, :],
                                                          op0=ALU.mult, op1=ALU.add)
                last.then_inc(s["x1"], 1)
                apart(dve, started)
                dve.wait_ge(s["x1"], g + 1)
                for b in range(PAIR):
                    last = nc.vector.bn_stats(st1[u][:, b, :], X[:, bass.ds(PAIR * g + b, 1), :])
                last.then_inc(s["xst"], 1)
                apart(dve, started)
                dve.wait_ge(s["xst"], g + 1)
                for b in range(PAIR):
                    last = nc.vector.bn_aggr(mv1[u][:, b, :], st1[u][:, b, :])
                last.then_inc(s["xmv"], 1)

            def norm1(g, u):
                dve.wait_ge(s["r1"], g + 1)
                wait(dve, s["xT2"], g - 1)
                wait(dve, s["xn1c"], g - 1)
                for b in range(PAIR):
                    last = nc.vector.tensor_scalar(xn1[u][:, b, :], X[:, bass.ds(PAIR * g + b, 1), :], mv1[u][:, b, 0:1],
                                                   r1[u][:, b:b + 1], ALU.subtract, ALU.mult)
                last.then_inc(s["xn1"], 1)

            pipeline(dve, NG, [(mask_bias, 0), (masked, 1), (norm, 0), (values, 0), (residual, 2), (norm1, 3), (attend_stats, 1)])

        @block.gpsimd
        def _(pool):

            def shifted(g, u):
                wait(pool, s["x1"], g - 1)
                nc.gpsimd.tensor_tensor(xb[u][:, :, :], X[:, bass.ds(PAIR * g, PAIR), :],
                                        shift[:, :].rearrange("p (o d) -> p o d", o=1).to_broadcast([128, PAIR, D]),
                                        ALU.add).then_inc(s["xb"], 1)

            def inv_std1(g, u):
                pool.wait_ge(s["xmv"], g + 1)
                wait(pool, s["xn1"], g - 1)
                nc.gpsimd.tensor_tensor(v1e[u][:, :], mv1[u][:, :, 1], eps[:, 0:1].to_broadcast([128, PAIR]), ALU.add).then_inc(s["vx"], 1)
                pool.wait_ge(s["vx"], g + 1)
                nc.gpsimd.tensor_tensor(r1[u][:, :], v1e[u][:, :], power[:, 0:PAIR], ALU.pow).then_inc(s["r1"], 1)

            def keep(g, u):
                pool.wait_ge(s["xn1"], g + 1)
                nc.gpsimd.tensor_copy(XN[:, bass.ds(PAIR * g, PAIR), :], xn1[u][:, :, :]).then_inc(s["xn1c"], 1)

            def inv_std0(g, u):
                pool.wait_ge(s["umv"], g + 1)
                wait(pool, s["x1"], g - 1)
                nc.gpsimd.tensor_tensor(vr[u][:, :], es[u][:, :], es[u][:, :], ALU.mult).then_inc(s["ves"], 1)
                pool.wait_ge(s["ves"], g + 1)
                nc.gpsimd.tensor_tensor(vr[u][:, :], vr[u][:, :], mv[u][:, :, 1], ALU.add).then_inc(s["uvr"], 1)
                pool.wait_ge(s["uvr"], g + 1)
                nc.gpsimd.tensor_tensor(ru[u][:, :], vr[u][:, :], power[:, 0:PAIR], ALU.pow).then_inc(s["vru"], 1)

            pipeline(pool, NG, [(shifted, 1), (inv_std1, 2), (keep, 3), (inv_std0, 1)])


@phase
def route(nc, sb, sem, sems, bank, m):
    X, XN, XNT, LG, ones, tri = (m[k] for k in ("X", "XN", "XNT", "LG", "ones", "tri"))
    rankrow, segments, tilestart = (m[k] for k in ("rankrow", "segments", "tilestart"))
    slot, tile_expert, sorted_x = (m[k] for k in ("slot", "tile_expert", "sorted_x"))
    wgs, wus, wds = (m[k] for k in ("wgs", "wus", "wds"))
    best = sb("best", [128, B])
    cand = sb("cand", [128, B, E])
    OH = sb("OH", [128, B, E])
    counts = sb("counts", [128, E, B])
    upto = sb("upto", [128, E, B])
    padi = sb("padi", [128, E], I32)
    pad = sb("pad", [128, E])
    ends = sb("ends", [128, E])
    where = sb("where", [128, B, E])
    slotf = sb("slotf", [128, B])
    past = sb("past", [1, NTILE, E])
    tef = sb("tef", [1, NTILE])
    sg = [sb(f"sg{c}", [128, 512]) for c in range(HC)]
    hT = [[sb(f"hT{u}{c}", [128, 512]) for c in range(HC)] for u in range(2)]
    s_r = sem("r_step")
    s_rank = sem("r_rank")
    s_slot = sem("r_slot")
    s_scat = sem("r_scat")
    s = sems("f", "hid silu hT down add")
    NC = B * S // 512
    bank_of = [(bank[0], bank[1]), (bank[2], bank[3])]
    bRank, bCount = bank[6], bank[7]

    with nc.Block() as block:
        @block.gpsimd
        def _(pool):
            pool.wait_ge(s_slot, 1)
            for b in range(B):
                nc.gpsimd.indirect_dma_start(sorted_x, bass.IndirectOffsetOnAxis(ap=slot[:, b:b + 1], axis=0),
                                             XN[:, b, :], None).then_inc(s_scat, 16)
            pool.wait_ge(s_scat, 16 * B)

        @block.tensor
        def _(pe):
            pe.wait_ge(s_r, 5)
            flat = OH[:, :, :].rearrange("p b e -> p (b e)")
            nc.tensor.matmul(bRank[:, 0:B * E], tri, flat, start=True, stop=True)
            nc.tensor.matmul(bCount[:, 0:B * E], ones[:, :], flat, start=True, stop=True).then_inc(s_rank, 1)

            def hidden(c, u):
                for k in range(HC):
                    gate, up = bank_of[k]
                    wait(pe, s["hT"], HC * (c - 1) + k + 1)
                    x = XNT[:, bass.ds(4 * c, 4), :]
                    nc.tensor.matmul(gate[:, :], wgs[:, k * 128:k * 128 + 128], x, start=True, stop=True)
                    nc.tensor.matmul(up[:, :], wus[:, k * 128:k * 128 + 128], x, start=True, stop=True).then_inc(s["hid"], 1)

            def down(c, u):
                pe.wait_ge(s["hT"], HC * c + HC)
                wait(pe, s["add"], c - 1)
                for t in range(4):
                    for k in range(HC):
                        last = nc.tensor.matmul(bank[4 + u][:, t * 128:t * 128 + 128], hT[u][k][:, t * 128:t * 128 + 128],
                                                wds[:, k, :], start=(k == 0), stop=(k == HC - 1))
                last.then_inc(s["down"], 1)

            pipeline(pe, NC, [(hidden, 0), (down, 1)])

        @block.scalar
        def _(act):
            def silu(c, u):
                for k in range(HC):
                    act.wait_ge(s["hid"], HC * c + k + 1)
                    wait(act, s["hT"], HC * (c - 1) + k + 1)
                    nc.scalar.activation(sg[k][:, :], bank_of[k][0][:, :], ACT.Silu).then_inc(s["silu"], 1)

            pipeline(act, NC, [(silu, 0)])

        @block.vector
        def _(dve):
            step = [0]

            def then(ins):
                step[0] += 1
                ins.then_inc(s_r, 1)
                dve.wait_ge(s_r, step[0])

            wide = lambda t: t.rearrange("p (b o) -> p b o", o=1).to_broadcast([128, B, E])
            then(nc.vector.tensor_reduce(best[:, :], LG[:, :, :], AX.X, ALU.max))
            then(nc.vector.tensor_tensor(cand[:, :, :], LG[:, :, :], wide(best[:, :]), ALU.is_equal))
            then(nc.vector.tensor_tensor(cand[:, :, :], cand[:, :, :],
                                         rankrow.rearrange("p (o e) -> p o e", o=1).to_broadcast([128, B, E]), ALU.mult))
            then(nc.vector.tensor_reduce(best[:, :], cand[:, :, :], AX.X, ALU.max))
            then(nc.vector.tensor_tensor(OH[:, :, :], cand[:, :, :], wide(best[:, :]), ALU.is_equal))
            dve.wait_ge(s_rank, 1)
            then(nc.vector.tensor_copy(counts[:, :, :], bCount[:, 0:B * E].rearrange("p (b e) -> p e b", e=E)))
            then(nc.vector.tensor_tensor_scan(upto[:, :, :].rearrange("p e b -> p (e b)"), segments,
                                              counts[:, :, :].rearrange("p e b -> p (e b)"), 0.0, ALU.mult, ALU.add))
            then(nc.vector.tensor_scalar(padi[:, :], upto[:, :, B - 1], 127.0, None, ALU.add))
            then(nc.vector.tensor_scalar(padi[:, :], padi[:, :], 7, 7, ALU.arith_shift_right, ALU.logical_shift_left))
            then(nc.vector.tensor_copy(pad[:, :], padi[:, :]))
            then(nc.vector.tensor_tensor_scan(ends[:, :], ones[:, 0:E], pad[:, :], 0.0, ALU.mult, ALU.add))
            then(nc.vector.tensor_tensor(pad[:, :], ends[:, :], pad[:, :], ALU.subtract))
            then(nc.vector.tensor_tensor(upto[:, :, :], upto[:, :, :], counts[:, :, :], ALU.subtract))
            then(nc.vector.tensor_tensor(upto[:, :, :], upto[:, :, :],
                                         pad[:, :].rearrange("p (e o) -> p e o", o=1).to_broadcast([128, E, B]), ALU.add))
            then(nc.vector.tensor_tensor(where[:, :, :], bRank[:, 0:B * E].rearrange("p (b e) -> p b e", e=E),
                                         upto[:, :, :].rearrange("p e b -> p b e"), ALU.add))
            then(nc.vector.tensor_tensor(where[:, :, :], where[:, :, :], OH[:, :, :], ALU.mult))
            then(nc.vector.tensor_reduce(slotf[:, :], where[:, :, :], AX.X, ALU.add))
            nc.vector.tensor_copy(slot[:, :], slotf[:, :]).then_inc(s_slot, 1)
            then(nc.vector.tensor_tensor(past[:, :, :], tilestart.rearrange("p (t o) -> p t o", o=1).to_broadcast([1, NTILE, E]),
                                         ends[0:1, :].rearrange("p (o e) -> p o e", o=1).to_broadcast([1, NTILE, E]), ALU.is_ge))
            then(nc.vector.tensor_reduce(tef[:, :], past[:, :, :], AX.X, ALU.add))
            then(nc.vector.tensor_scalar(tile_expert[:, :], tef[:, :], float(E - 1), None, ALU.min))

            def product(c, u):
                for k in range(HC):
                    dve.wait_ge(s["silu"], HC * c + k + 1)
                    wait(dve, s["down"], c - 1)
                    nc.vector.tensor_tensor(hT[u][k][:, :], sg[k][:, :], bank_of[k][1][:, :], ALU.mult).then_inc(s["hT"], 1)

            def add(c, u):
                dve.wait_ge(s["down"], c + 1)
                x = X[:, bass.ds(4 * c, 4), :]
                nc.vector.tensor_tensor(x, x, bank[4 + u][:, :].rearrange("p (b d) -> p b d", b=4), ALU.add).then_inc(s["add"], 1)

            pipeline(dve, NC, [(product, 0), (add, 1)])


@phase
def experts(nc, sb, sem, sems, bank, m):
    ident, tile_expert, sorted_x, sorted_y = (m[k] for k in ("ident", "tile_expert", "sorted_x", "sorted_y"))
    wgu, wdn = m["wgu"], m["wdn"]
    two = range(2)
    xs = [sb(f"xs{u}", [128, D]) for u in two]
    xsT = [sb(f"xsT{u}", [128, 128]) for u in two]
    act_g = [sb(f"actg{u}", [128, H]) for u in two]
    hid = [sb(f"hid{u}", [128, H]) for u in two]
    hidT = [sb(f"hidT{u}", [128, HC, 128]) for u in two]
    ys = [sb(f"ys{u}", [128, D]) for u in two]
    l_x = [sem(f"e_x{u}") for u in two]
    st_y = [sem(f"e_y{u}") for u in two]
    s = sems("e", "xT xTs h silu hid hT hTs y ys")
    bX, bH, bHT, bY = bank[0:2], bank[2:4], bank[4:6], bank[6:8]
    rows = lambda t, i: t.rearrange("(t p) d -> t p d", p=128)[bass.ds(i, 1)].rearrange("o p d -> (o p) d")

    with nc.Block() as block:
        @block.sync
        def _(sp):
            def load(t, u):
                wait(sp, s["xT"], t - 1)
                sp.dma_start(xs[u][:, :], rows(sorted_x, t)).then_inc(l_x[u], 16)

            def store(t, u):
                sp.wait_ge(s["ys"], t + 1)
                sp.dma_start(rows(sorted_y, t), ys[u][:, :]).then_inc(st_y[u], 16)

            pipeline(sp, NTILE, [(load, 0), (store, 5)])
            for u in two:
                sp.wait_ge(st_y[u], 8 * NTILE)

        @block.tensor
        def _(pe):
            def rows_T(t, u):
                landed(pe, l_x, t, u)
                wait(pe, s["xTs"], t - 1)
                nc.tensor.transpose(bX[u][:, 0:128], xs[u][:, :], ident).then_inc(s["xT"], 1)

            def up(t, u):
                pe.wait_ge(s["xTs"], t + 1)
                wait(pe, s["hid"], t - 1)
                e = nc.tensor.value_load(tile_expert[0:1, bass.ds(t, 1)], min_val=0, max_val=E - 1)
                nc.tensor.matmul(bH[u][:, :], xsT[u][:, :], wgu[:, bass.ds(e, 1), :], start=True, stop=True).then_inc(s["h"], 1)

            def hidden_T(t, u):
                pe.wait_ge(s["hid"], t + 1)
                wait(pe, s["hTs"], t - 1)
                for k in range(HC):
                    last = nc.tensor.transpose(bHT[u][:, k * 128:k * 128 + 128], hid[u][:, k * 128:k * 128 + 128], ident)
                last.then_inc(s["hT"], 1)

            def down(t, u):
                pe.wait_ge(s["hTs"], t + 1)
                wait(pe, s["ys"], t - 1)
                e = nc.tensor.value_load(tile_expert[0:1, bass.ds(t, 1)], min_val=0, max_val=E - 1)
                for k in range(HC):
                    last = nc.tensor.matmul(bY[u][:, 0:D], hidT[u][:, k, :], wdn[:, bass.ds(e, 1), k, :],
                                            start=(k == 0), stop=(k == HC - 1))
                last.then_inc(s["y"], 1)

            pipeline(pe, NTILE, [(rows_T, 0), (hidden_T, 2), (up, 1), (down, 3)])

        @block.scalar
        def _(act):
            def rows_T(t, u):
                act.wait_ge(s["xT"], t + 1)
                wait(act, s["h"], t - 1)
                nc.scalar.activation(xsT[u][:, :], bX[u][:, 0:128], ACT.Copy).then_inc(s["xTs"], 1)

            def silu(t, u):
                act.wait_ge(s["h"], t + 1)
                wait(act, s["hid"], t - 1)
                nc.scalar.activation(act_g[u][:, :], bH[u][:, 0:H], ACT.Silu).then_inc(s["silu"], 1)

            def hidden_T(t, u):
                act.wait_ge(s["hT"], t + 1)
                wait(act, s["y"], t - 1)
                nc.scalar.activation(hidT[u][:, :, :].rearrange("p k t -> p (k t)"), bHT[u][:, 0:H], ACT.Copy).then_inc(s["hTs"], 1)

            pipeline(act, NTILE, [(rows_T, 0), (hidden_T, 2), (silu, 1)])

        @block.vector
        def _(dve):
            def product(t, u):
                dve.wait_ge(s["silu"], t + 1)
                wait(dve, s["hT"], t - 1)
                nc.vector.tensor_tensor(hid[u][:, :], act_g[u][:, :], bH[u][:, H:2 * H], ALU.mult).then_inc(s["hid"], 1)

            def result(t, u):
                dve.wait_ge(s["y"], t + 1)
                if not (isinstance(t, int) and t < 2):
                    dve.wait_ge(st_y[u], 8 * (t - u))
                nc.vector.tensor_copy(ys[u][:, :], bY[u][:, 0:D]).then_inc(s["ys"], 1)

            pipeline(dve, NTILE, [(product, 1), (result, 3)])


@phase
def collect(nc, sb, sem, sems, bank, m):
    XN, slot, sorted_y = m["XN"], m["slot"], m["sorted_y"]
    s_g = sem("g_rows")
    with nc.Block() as block:
        @block.gpsimd
        def _(pool):
            for b in range(B):
                nc.gpsimd.indirect_dma_start(XN[:, b, :], None, sorted_y,
                                             bass.IndirectOffsetOnAxis(ap=slot[:, b:b + 1], axis=0)).then_inc(s_g, 16)
            pool.wait_ge(s_g, 16 * B)


@phase
def attend_1(nc, sb, sem, sems, bank, out, m):
    X, Y, K1T, V1, power, ident, ones = (m[k] for k in ("X", "XN", "K1T", "V1", "power", "ident", "ones"))
    identb, selb, headmask, biasT, biasQ = (m[k] for k in ("identb", "selb", "headmask", "biasT", "biasQ"))
    padT, padR, onesb, zeros = m["padT"], m["padR"], m["onesb"], m["zeros"]
    wq1, qscale, qbias, wo1, bo1 = (m[k] for k in ("wq1", "qscale", "qbias", "wo1", "bo1"))
    sgn, w2, b2, rankrow = (m[k] for k in ("sgn", "w2", "b2", "rankrow"))
    started, eps = m["s_set"], m["eps"]
    two = range(2)
    x2 = [sb(f"x2{u}", [128, D]) for u in two]
    x2b = [sb(f"x2b{u}", [128, D]) for u in two]
    st2 = [sb(f"st2{u}", [128, 6]) for u in two]
    mv2 = [sb(f"mv2{u}", [128, 2]) for u in two]
    v2e = [sb(f"v2e{u}", [128, 1]) for u in two]
    r2 = [sb(f"r2{u}", [128, 1]) for u in two]
    xn2 = [sb(f"xn2{u}", [128, D]) for u in two]
    xn2T = [sb(f"xn2T{u}", [128, S]) for u in two]
    QT = [sb(f"QT{u}", [128, S]) for u in two]
    KB = [sb(f"KB{u}", [128, NH, SK]) for u in two]
    VP = [sb(f"VP{u}", [SK, NH, 32]) for u in two]
    pad = [sb(f"pad{u}", [SK, 1]) for u in two]
    nmax, dead = m["nmax"], sb("dead", [128, B])
    nm = [sb(f"nm{u}", [128, NH], BF16) for u in two]
    nmT = [sb(f"nmT{u}", [NH, S], BF16) for u in two]
    SB = [sb(f"SB{u}", [SK, HG * S]) for u in two]
    PE_ = [sb(f"PE{u}", [SK, HG * S]) for u in two]
    OS = [sb(f"OS{u}", [128, NCH, S]) for u in two]
    rden = [sb(f"rden{u}", [128, NCH, HG]) for u in two]
    AO = [sb(f"AO{u}", [128, D]) for u in two]
    AOT = [sb(f"AOT{u}", [128, S]) for u in two]
    x3 = [sb(f"x3{u}", [128, D]) for u in two]
    st3 = [sb(f"st3{u}", [128, 6]) for u in two]
    mv3 = [sb(f"mv3{u}", [128, 2]) for u in two]
    v3e = [sb(f"v3e{u}", [128, 1]) for u in two]
    r3 = [sb(f"r3{u}", [128, 1]) for u in two]
    xn3 = [sb(f"xn3{u}", [128, D]) for u in two]
    xn3T = [sb(f"xn3T{u}", [128, S]) for u in two]
    am = [sb(f"am{u}", [128, 4, T]) for u in two]
    OH = [sb(f"OH{u}", [128, T]) for u in two]
    OHT = [sb(f"OHT{u}", [T, S]) for u in two]
    picked = [sb(f"picked{u}", [128, T, D]) for u in two]
    sum4 = [sb(f"sum4{u}", [128, 4, D]) for u in two]
    x3b = [sb(f"x3b{u}", [128, D]) for u in two]
    res = [sb(f"res{u}", [128, D]) for u in two]

    bM, bSc, bO, bA, bB, bF = bank[0:2], bank[2:4], bank[4], bank[5], bank[6], bank[7]
    HT = T // 2
    s = sems("d", "set clear pd x2 x2b st2 mv2 v2 r2 xn2 xT xTs q qs kb vp ms mx nT nTs sc sb ex pv os oT "
                  "rd ao aT aTs y x3 st3 mv3 v3 r3 xn3 zT zTs sg am oh hT hTs f pk fb x3b s4 s2 s1 res")
    st_o = [sem(f"d_out{u}") for u in two]
    N = NCH

    with nc.Block() as block:
        @block.tensor
        def _(pe):
            pe.wait_ge(s["set"], 1)

            def norm_T(b, u):
                pe.wait_ge(s["xn2"], b + 1)
                wait(pe, s["x3b"], b - 2)
                nc.tensor.transpose(bA[:, 0:128], xn2[u][:, :], ident).then_inc(s["xT"], 1)

            def queries(b, u):
                pe.wait_ge(s["xTs"], b + 1)
                nc.tensor.matmul(bA[:, 0:128], wq1[:, :], xn2T[u][:, :], start=True, stop=True).then_inc(s["q"], 1)

            def max_scores(c):
                def stage(b, u):
                    pe.wait_ge(s["qs"], b + 1)
                    pe.wait_ge(s["kb"], b + 1)
                    wait(pe, s["mx"], N * b + c - 1)
                    o = bM[c % 2][:, 0:HG * SK]
                    nc.tensor.matmul(o, QT[u][:, :], KB[u][:, c * HG:(c + 1) * HG, :], start=True, stop=False)
                    nc.tensor.matmul(o, onesb[:, :], padR[:, bass.ds(b, 1), :].to_broadcast([1, HG, SK]), start=False, stop=False)
                    nc.tensor.matmul(o, identb[:, :], biasQ[:, c * HG:(c + 1) * HG, :], start=False, stop=True).then_inc(s["ms"], 1)
                return stage

            def max_T(b, u):
                pe.wait_ge(s["mx"], N * (b + 1))
                nc.tensor.matmul(bA[0:NH, 0:128], nm[u][:, :], identb[:, :], start=True, stop=True).then_inc(s["nT"], 1)

            def scores(c):
                def stage(b, u):
                    pe.wait_ge(s["nTs"], b + 1)
                    wait(pe, s["sb"], N * b + c - 1)
                    for j in range(HG):
                        h = c * HG + j
                        o = bSc[c % 2][0:SK, j * 128:j * 128 + 128]
                        nc.tensor.matmul(o, KB[u][:, h, :], QT[u][:, :], start=True, stop=False)
                        last = nc.tensor.matmul(o, selb[:, h, :], nmT[u][:, :], start=False, stop=True)
                    last.then_inc(s["sc"], 1)
                return stage

            def weigh(c):
                def stage(b, u):
                    pe.wait_ge(s["ex"], N * b + c + 1)
                    pe.wait_ge(s["vp"], b + 1)
                    if c == 0:
                        wait(pe, s["os"], b)
                    for j in range(HG):
                        last = nc.tensor.matmul(bO[32 * j:32 * j + 32, c * 128:c * 128 + 128], VP[u][:, c * HG + j, :],
                                                PE_[c % 2][:, j * 128:j * 128 + 128], start=True, stop=True)
                    last.then_inc(s["pv"], 1)
                return stage

            def heads_T(b, u):
                pe.wait_ge(s["os"], b + 1)
                wait(pe, s["x3"], b)
                for c in range(NCH):
                    last = nc.tensor.transpose(bB[:, c * 128:c * 128 + 128], OS[u][:, c, :], ident)
                last.then_inc(s["oT"], 1)

            def mixed_T(b, u):
                pe.wait_ge(s["ao"], b + 1)
                nc.tensor.transpose(bB[:, 0:128], AO[u][:, :], ident).then_inc(s["aT"], 1)

            def project(b, u):
                pe.wait_ge(s["aTs"], b + 1)
                nc.tensor.matmul(bB[:, 0:128], AOT[u][:, :], wo1[:, :], start=True, stop=True).then_inc(s["y"], 1)

            def norm3_T(b, u):
                pe.wait_ge(s["xn3"], b + 1)
                wait(pe, s["pk"], 2 * b)
                nc.tensor.transpose(bF[:, 0:128], xn3[u][:, :], ident).then_inc(s["zT"], 1)

            def signature(b, u):
                pe.wait_ge(s["zTs"], b + 1)
                nc.tensor.matmul(bF[:, 0:T], xn3T[u][:, :], sgn[:, :], start=True, stop=True).then_inc(s["sg"], 1)

            def maps(k):
                def stage(b, u):
                    if k == 0:
                        pe.wait_ge(s["oh"], b + 1)
                    else:
                        pe.wait_ge(s["pk"], 2 * b + 1)
                    nc.tensor.matmul(bF[:, :], xn3T[u][:, :], w2[:, k * HT:(k + 1) * HT, :], start=True, stop=True).then_inc(s["f"], 1)
                return stage

            def choice_T(b, u):
                pe.wait_ge(s["oh"], b + 1)
                wait(pe, s["x3b"], b)
                nc.tensor.transpose(bA[0:T, 0:128], OH[u][:, :], ident).then_inc(s["hT"], 1)

            def picked_bias(b, u):
                pe.wait_ge(s["hTs"], b + 1)
                nc.tensor.matmul(bA[:, 0:128], OHT[u][:, :], b2[:, :], start=True, stop=True).then_inc(s["fb"], 1)

            def after_max_T(b, u):
                pe.wait_ge(s["nTs"], b + 1)

            pipeline(pe, B, [
                (norm_T, 0), (scores(0), 1), (scores(1), 1), (queries, 0), (weigh(0), 1), (scores(2), 1),
                (max_scores(0), 0), (weigh(1), 1), (scores(3), 1), (max_scores(1), 0), (weigh(2), 1),
                (norm3_T, 2), (max_scores(2), 0), (weigh(3), 1), (signature, 2), (max_scores(3), 0),
                (heads_T, 1), (max_T, 0), (maps(0), 2), (mixed_T, 1), (after_max_T, 0), (choice_T, 2),
                (maps(1), 2), (picked_bias, 2), (project, 1)])

        @block.scalar
        def _(act):

            def norm_T(b, u):
                act.wait_ge(s["xT"], b + 1)
                wait(act, s["q"], b - 1)
                nc.scalar.activation(xn2T[u][:, :], bA[:, 0:128], ACT.Copy).then_inc(s["xTs"], 1)

            def queries(b, u):
                act.wait_ge(s["q"], b + 1)
                wait(act, s["sc"], N * (b - 1))
                nc.scalar.activation(QT[u][:, :], bA[:, 0:128], ACT.Identity, bias=qbias[:, 0:1],
                                     scale=qscale[:, 0:1]).then_inc(s["qs"], 1)

            def max_T(b, u):
                act.wait_ge(s["nT"], b + 1)
                wait(act, s["sc"], N * (b - 1))
                nc.scalar.activation(nmT[u][:, :], bA[0:NH, 0:128], ACT.Copy).then_inc(s["nTs"], 1)

            def exps(c):
                def stage(b, u):
                    act.wait_ge(s["sb"], N * b + c + 1)
                    act.wait_ge(s["pd"], b + 1)
                    wait(act, s["pv"], N * b + c - 1)
                    nc.scalar.activation(PE_[c % 2][:, :], SB[c % 2][:, :], ACT.Exp, bias=pad[u][:, 0:1]).then_inc(s["ex"], 1)
                return stage

            def heads(b, u):
                act.wait_ge(s["pv"], N * (b + 1))
                wait(act, s["oT"], b - 1)
                nc.scalar.activation(OS[u][:, :, :].rearrange("p c s -> p (c s)"), bO[:, :], ACT.Copy).then_inc(s["os"], 1)

            def mixed_T(b, u):
                act.wait_ge(s["aT"], b + 1)
                wait(act, s["y"], b - 1)
                nc.scalar.activation(AOT[u][:, :], bB[:, 0:128], ACT.Copy).then_inc(s["aTs"], 1)

            def norm3_T(b, u):
                act.wait_ge(s["zT"], b + 1)
                wait(act, s["f"], 2 * (b - 1))
                nc.scalar.activation(xn3T[u][:, :], bF[:, 0:128], ACT.Copy).then_inc(s["zTs"], 1)

            def choice_T(b, u):
                act.wait_ge(s["hT"], b + 1)
                wait(act, s["fb"], b - 1)
                nc.scalar.activation(OHT[u][:, :], bA[0:T, 0:128], ACT.Copy).then_inc(s["hTs"], 1)

            pipeline(act, B, [
                (norm_T, 0), (exps(0), 1), (queries, 0), (exps(1), 1), (exps(2), 1), (exps(3), 1), (norm3_T, 2),
                (heads, 1), (max_T, 0), (mixed_T, 1), (choice_T, 2)])

        @block.vector
        def _(dve):
            for u in two:
                nc.vector.memset(VP[u][:, :, :], 0.0).then_inc(s["clear"], 1)
            dve.wait_ge(s["clear"], 2)
            for u in two:
                last = nc.vector.memset(VP[u][:, :, HD:HD + 1], 1.0)
            last.then_inc(s["set"], 1)
            nc.vector.tensor_scalar(dead[:, :], nmax[:, :], 4.0, 0.0, ALU.mult, ALU.mult).then_inc(s["clear"], 1)
            dve.wait_ge(s["clear"], 3)

            def stats2(b, u):
                apart(dve, started)
                dve.wait_ge(s["x2"], b + 1)
                wait(dve, s["r2"], b - 1)
                nc.vector.bn_stats(st2[u][:, :], x2[u][:, :]).then_inc(s["st2"], 1)
                apart(dve, started)
                dve.wait_ge(s["st2"], b + 1)
                nc.vector.bn_aggr(mv2[u][:, :], st2[u][:, :]).then_inc(s["mv2"], 1)

            def norm2(b, u):
                dve.wait_ge(s["r2"], b + 1)
                dve.wait_ge(s["mv2"], b + 1)
                wait(dve, s["xT"], b - 1)
                nc.vector.tensor_scalar(xn2[u][:, :], x2[u][:, :], mv2[u][:, 0:1], r2[u][:, 0:1],
                                        ALU.subtract, ALU.mult).then_inc(s["xn2"], 1)

            def maxima(c):
                def stage(b, u):
                    dve.wait_ge(s["ms"], N * b + c + 1)
                    if c == 0:
                        wait(dve, s["nT"], b - 1)
                    nc.vector.tensor_reduce(nm[u][:, c * HG:(c + 1) * HG],
                                            bM[c % 2][:, 0:HG * SK].rearrange("p (h k) -> p h k", h=HG),
                                            AX.X, ALU.max, negate=True).then_inc(s["mx"], 1)
                return stage

            def bias(c):
                def stage(b, u):
                    dve.wait_ge(s["sc"], N * b + c + 1)
                    wait(dve, s["ex"], N * b + c - 1)
                    nc.vector.tensor_tensor(SB[c % 2][:, :], bSc[c % 2][0:SK, :],
                                            biasT[:, c * HG:(c + 1) * HG, :].rearrange("k h q -> k (h q)"),
                                            ALU.add).then_inc(s["sb"], 1)
                return stage

            def mix(b, u):
                dve.wait_ge(s["oT"], b + 1)
                wait(dve, s["aT"], b - 1)
                v = bB[:, :].rearrange("p (c j r) -> p c j r", c=NCH, j=HG)
                nc.vector.reciprocal(rden[u][:, :, :], v[:, :, :, HD]).then_inc(s["rd"], 1)
                dve.wait_ge(s["rd"], b + 1)
                nc.vector.tensor_tensor(AO[u][:, :].rearrange("p (c j r) -> p c j r", c=NCH, j=HG), v[:, :, :, 0:HD],
                                        rden[u][:, :, :].rearrange("p c (j o) -> p c j o", o=1).to_broadcast([128, NCH, HG, HD]),
                                        ALU.mult).then_inc(s["ao"], 1)

            def residual(b, u):
                dve.wait_ge(s["y"], b + 1)
                dve.wait_ge(s["x2b"], b + 1)
                wait(dve, s["x3b"], b - 1)
                wait(dve, s["r3"], b - 1)
                nc.vector.tensor_tensor(x3[u][:, :], bB[:, 0:128], x2b[u][:, :], ALU.add).then_inc(s["x3"], 1)
                dve.wait_ge(s["x3"], b + 1)
                nc.vector.bn_stats(st3[u][:, :], x3[u][:, :]).then_inc(s["st3"], 1)
                apart(dve, started)
                dve.wait_ge(s["st3"], b + 1)
                nc.vector.bn_aggr(mv3[u][:, :], st3[u][:, :]).then_inc(s["mv3"], 1)

            def norm3(b, u):
                dve.wait_ge(s["r3"], b + 1)
                dve.wait_ge(s["mv3"], b + 1)
                wait(dve, s["zT"], b - 1)
                nc.vector.tensor_scalar(xn3[u][:, :], x3[u][:, :], mv3[u][:, 0:1], r3[u][:, 0:1],
                                        ALU.subtract, ALU.mult).then_inc(s["xn3"], 1)

            def choose(b, u):
                dve.wait_ge(s["sg"], b + 1)
                wait(dve, s["hT"], b - 1)
                t = am[u]
                n = 3 * b
                nc.vector.tensor_reduce(t[:, 0, 0:1], bF[:, 0:T], AX.X, ALU.max).then_inc(s["am"], 1)
                dve.wait_ge(s["am"], n + 1)
                nc.vector.scalar_tensor_tensor(out=t[:, 1, :], in0=bF[:, 0:T], scalar=t[:, 0, 0:1], in1=rankrow,
                                               op0=ALU.is_equal, op1=ALU.mult).then_inc(s["am"], 1)
                dve.wait_ge(s["am"], n + 2)
                nc.vector.tensor_reduce(t[:, 2, 0:1], t[:, 1, :], AX.X, ALU.max).then_inc(s["am"], 1)
                dve.wait_ge(s["am"], n + 3)
                nc.vector.tensor_scalar(OH[u][:, :], t[:, 1, :], t[:, 2, 0:1], None, ALU.is_equal).then_inc(s["oh"], 1)

            def pick(k):
                def stage(b, u):
                    dve.wait_ge(s["f"], 2 * b + k + 1)
                    dve.wait_ge(s["oh"], b + 1)
                    wait(dve, s["s4"], b - 1)
                    nc.vector.tensor_tensor(picked[u][:, k * HT:(k + 1) * HT, :],
                                            bF[:, :].rearrange("p (t d) -> p t d", t=HT),
                                            OH[u][:, k * HT:(k + 1) * HT].rearrange("p (t o) -> p t o", o=1).to_broadcast([128, HT, D]),
                                            ALU.mult).then_inc(s["pk"], 1)
                return stage

            def add_bias(b, u):
                dve.wait_ge(s["fb"], b + 1)
                wait(dve, s["res"], b - 1)
                nc.vector.scalar_tensor_tensor(out=x3b[u][:, :], in0=bA[:, 0:128], scalar=dead[:, bass.ds(b, 1)],
                                               in1=x3[u][:, :], op0=ALU.add, op1=ALU.add).then_inc(s["x3b"], 1)

            pipeline(dve, B, [
                (norm2, 0), (bias(0), 1), (bias(1), 1), (bias(2), 1), (maxima(0), 0), (norm3, 2), (bias(3), 1), (maxima(1), 0),
                (maxima(2), 0), (choose, 2), (maxima(3), 0), (stats2, -1), (mix, 1), (pick(0), 2), (pick(1), 2),
                (add_bias, 2), (residual, 1)])

        @block.gpsimd
        def _(pool):
            pool.wait_ge(s["set"], 1)
            none = zeros[0:SK, 0:1]

            def keys(b, u):
                wait(pool, s["sc"], N * (b - 1))
                nc.gpsimd.tensor_tensor(KB[u][:, :, :], K1T[:, bass.ds(b, 1), :].to_broadcast([128, NH, SK]),
                                        headmask.rearrange("p (h o) -> p h o", o=1).to_broadcast([128, NH, SK]),
                                        ALU.mult).then_inc(s["kb"], 1)

            def values(b, u):
                wait(pool, s["pv"], N * (b - 1))
                nc.gpsimd.tensor_copy(VP[u][:, :, 0:HD],
                                      V1[:, bass.ds(b, 1), :].rearrange("k o (h d) -> k (o h) d", h=NH)).then_inc(s["vp"], 1)

                nc.gpsimd.tensor_tensor(pad[u][:, :], padT[:, bass.ds(b, 1)], none, ALU.add).then_inc(s["pd"], 1)

            def stream(b, u):
                wait(pool, s["xn2"], b - 1)
                wait(pool, s["x2b"], b - 1)
                nc.gpsimd.tensor_tensor(x2[u][:, :].rearrange("p (o d) -> p o d", o=1), X[:, bass.ds(b, 1), :],
                                        Y[:, bass.ds(b, 1), :], ALU.add).then_inc(s["x2"], 1)

            def with_bias(b, u):
                pool.wait_ge(s["x2"], b + 1)
                wait(pool, s["x3"], b - 1)
                nc.gpsimd.tensor_tensor(x2b[u][:, :], x2[u][:, :], bo1[:, :], ALU.add).then_inc(s["x2b"], 1)

            def inv_std(x):
                mv, ve, r, ready, mid, done, used = x

                def stage(b, u):
                    pool.wait_ge(s[ready], b + 1)
                    wait(pool, s[used], b - 1)
                    nc.gpsimd.tensor_tensor(ve[u][:, :], mv[u][:, 1:2], eps[:, :], ALU.add).then_inc(s[mid], 1)
                    pool.wait_ge(s[mid], b + 1)
                    nc.gpsimd.tensor_tensor(r[u][:, :], ve[u][:, :], power[:, 0:1], ALU.pow).then_inc(s[done], 1)
                return stage

            inv2 = inv_std((mv2, v2e, r2, "mv2", "v2", "r2", "xn2"))
            inv3 = inv_std((mv3, v3e, r3, "mv3", "v3", "r3", "xn3"))

            def total(b, u):
                pool.wait_ge(s["pk"], 2 * b + 2)
                nc.gpsimd.tensor_tensor(sum4[u][:, :, :], picked[u][:, 0:4, :], picked[u][:, 4:8, :], ALU.add).then_inc(s["s4"], 1)
                pool.wait_ge(s["s4"], b + 1)
                nc.gpsimd.tensor_tensor(sum4[u][:, 0:2, :], sum4[u][:, 0:2, :], sum4[u][:, 2:4, :], ALU.add).then_inc(s["s2"], 1)
                pool.wait_ge(s["s2"], b + 1)
                nc.gpsimd.tensor_tensor(sum4[u][:, 0, :], sum4[u][:, 0, :], sum4[u][:, 1, :], ALU.add).then_inc(s["s1"], 1)
                pool.wait_ge(s["s1"], b + 1)
                pool.wait_ge(s["x3b"], b + 1)
                if not (isinstance(b, int) and b < 2):
                    pool.wait_ge(st_o[u], 8 * (b - u))
                nc.gpsimd.tensor_tensor(res[u][:, :], sum4[u][:, 0, :], x3b[u][:, :], ALU.add).then_inc(s["res"], 1)

            pipeline(pool, B, [(values, -1), (with_bias, 0), (stream, -2), (inv2, -1), (total, 3), (inv3, 1), (keys, -1)])

        @block.sync
        def _(sp):
            def store(b, u):
                sp.wait_ge(s["res"], b + 1)
                sp.dma_start(out[bass.ds(b, 1)].rearrange("o s d -> (o s) d"), res[u][:, :]).then_inc(st_o[u], 16)

            pipeline(sp, B, [(store, 0)])
            for u in two:
                sp.wait_ge(st_o[u], 8 * B)


def kernel(**inputs):
    import concourse.bacc as _bacc
    from concourse.bass_utils import run_bass_kernel_spmd as _run

    def i(name):
        return np.asarray(inputs[name])

    table = i("L1_xattn_bias_table").T
    arrays = {
        "x": i("x"),
        "ctxT": i("ctx_1024").transpose(2, 0, 1).reshape(D, NG, PAIR * SK),
        "mask": i("mask_BxSxS2_ik1").transpose(1, 0, 2),
        "wqT0": i("L0_xattn_Wq").T, "wkT0": i("L0_xattn_Wk").T, "wv0": i("L0_xattn_Wv"), "wv1": i("L1_xattn_Wv"),
        "bq0": i("L0_xattn_bq"), "bk0": i("L0_xattn_bk"), "bv0": i("L0_xattn_bv"),
        "gamma": i("L0_xattn_ln_gamma"), "beta": i("L0_xattn_ln_beta"),
        "bq1": i("L1_xattn_bq"), "bk1": i("L1_xattn_bk"), "bv1": i("L1_xattn_bv"), "bo1": i("L1_xattn_bo"),
        "g_xattn": i("g_xattn"), "g_ffn": i("g_ffn"),
        "logit_scale": np.repeat(i("L1_xattn_logit_scale"), HD),
        "wk1": i("L1_xattn_Wk"), "wq1": i("L1_xattn_Wq"), "wo1": i("L1_xattn_Wo"),
        "router": i("L0_ffn_router").T, "wgs": i("L0_ffn_w_gate_s").T, "wus": i("L0_ffn_w_up_s").T,
        "wds": i("L0_ffn_w_down_s").T.reshape(HC, 128, D).transpose(1, 0, 2),
        "wgu": np.concatenate([i("L0_ffn_gate"), i("L0_ffn_up")], axis=1).transpose(2, 0, 1),
        "wdn": i("L0_ffn_down").transpose(2, 0, 1).reshape(HC, 128, E, D).transpose(1, 2, 0, 3),
        "sigs": i("L1_ffn_tile_sigs").T, "w2": i("L1_ffn_W").transpose(1, 0, 2), "b2": i("L1_ffn_b"),
        "pad": i("mask_BxS2_bf0").reshape(-1), "padT": i("mask_BxS2_bf0").T,
        "table": table, "table_rev": table[:, ::-1],
        "cst": constants(),
    }
    nc = _bacc.Bacc("TRN2", target_bir_lowering=False, num_devices=1)
    feed, aps = {}, {}
    for name, v in arrays.items():
        feed[f"in_{name}"] = np.ascontiguousarray(v)
        aps[name] = nc.dram_tensor(f"in_{name}", v.shape, mybir.dt.from_np(v.dtype), kind="ExternalInput").ap()
    out = nc.dram_tensor("out_0", (B, S, D), F32, kind="ExternalOutput").ap()
    build(nc, aps, out)
    return _run(nc, [feed], core_ids=[0]).results[0]["out_0"]
```

```python
from contextlib import ExitStack

import concourse.bass as bass
import numpy as np
from concourse import mybir

F32 = mybir.dt.float32
BF16 = mybir.dt.bfloat16
I32 = mybir.dt.int32
U32 = mybir.dt.uint32
U8 = mybir.dt.uint8
ALU = mybir.AluOpType
ACT = mybir.ActivationFunctionType
AX = mybir.AxisListType

B, S, D = 32, 128, 128
SK = 77
E, H = 8, 256
HC = H // 128
NH, HD = 16, 8
HG = 4
NCH = NH // HG
T = 8
NTILE = 40
SLOTS = NTILE * 128
SPARE = 512
UP, DOWN = 1, 4
TURNS = (NTILE + DOWN) // 2
PAIR = 2
NG = B // PAIR
EPS = 1e-5
NEG = -3.0e38
PADDED = -(2.0 ** 100)

C_IDENT = 0
C_TRI = C_IDENT + 128
C_HEAD = C_TRI + 128
C_RANK = C_HEAD + NH
C_SEG = C_RANK + E
C_TILE = C_SEG + E * B
C_ROW = C_TILE + NTILE
C_SPARE = C_ROW + B
C_END = C_SPARE + 4


def constants():
    c = np.zeros((128, C_END), np.float32)
    p = np.arange(128)
    c[:, C_IDENT:C_TRI] = np.eye(128)
    c[:, C_TRI:C_HEAD] = p[:, None] < p[None, :]
    c[:, C_HEAD:C_RANK] = p[:, None] // HD == np.arange(NH)[None, :]
    c[:, C_RANK:C_SEG] = E - np.arange(E)
    c[:, C_SEG:C_TILE] = np.arange(E * B) % B != 0
    c[:, C_TILE:C_ROW] = 128 * np.arange(NTILE)
    c[:, C_ROW:C_SPARE] = SPARE + 128 * np.arange(B)[None, :] + p[:, None]
    r = 4 * p[:, None] + np.arange(4)[None, :]
    c[:, C_SPARE:C_END] = r % SPARE
    return c


def wait(eng, sem, value):
    if isinstance(value, int) and value <= 0:
        return
    eng.wait_ge(sem, value)


def apart(eng, started):
    eng.wait_ge(started, 1)


def pipeline(eng, n, stages, ways=2, begin=None):
    first = min(lag for _, lag in stages)
    stages = [(stage, lag - first) for stage, lag in stages]
    span = max(lag for _, lag in stages)
    head = -(-(span + ways) // ways)
    tail = -(-(n + span) // ways)

    def turn(i):
        if begin:
            begin(i)
        for u in range(ways):
            for stage, lag in stages:
                item = ways * i + u - lag
                if isinstance(item, int) and not 0 <= item < n:
                    continue
                stage(item, (u - lag) % ways)

    for i in range(head):
        turn(i)
    with eng.Fori(head, n // ways) as i:
        turn(i)
    for i in range(n // ways, tail):
        turn(i)


def landed(eng, sems, item, way):
    eng.wait_ge(sems[way], 16 // len(sems) * (item - way) + 16)


def free(eng, sems, item, way):
    if not (isinstance(item, int) and item < len(sems)):
        eng.wait_ge(sems[way], 16 // len(sems) * (item - way))


def phase(f):
    def run(nc, *rest):
        with ExitStack() as own:
            def sb(name, shape, dt=F32):
                return own.enter_context(nc.sbuf_tensor(name, shape, dt))
            f(nc, sb, *rest)
    return run


def build(nc, a, out):
    with ExitStack() as ctx:
        def sb(name, shape, dt=F32):
            return ctx.enter_context(nc.sbuf_tensor(name, shape, dt))

        def sem(name):
            return ctx.enter_context(nc.semaphore(name))

        def sems(stem, names):
            return {n: sem(f"{stem}_{n}") for n in names.split()}

        bank = [ctx.enter_context(nc.psum_tensor(f"bank{i}", [128, 512], F32)) for i in range(8)]

        sorted_x = nc.dram_tensor("sorted_x", (SLOTS, D + 1), F32).ap()
        routed = nc.dram_tensor("routed", (SPARE + B * S, D), F32).ap()
        wide_qk = nc.dram_tensor("wide_qk", (NH, S, SK), F32).ap()

        X = sb("X", [128, B, D])
        LG = sb("LG", [128, B, E])
        XN = sb("XN", [128, B, D + 1])
        XNT = sb("XNT", [128, B, S])
        K1T = sb("K1T", [128, B, SK])
        V1 = sb("V1", [SK, B, D])
        stats0 = sb("stats0", [128, B, 6])
        nmean0 = sb("nmean0", [128, B])
        nb0 = sb("nb0", [128, B])
        var0 = sb("var0", [128, B])
        rstd0 = sb("rstd0", [128, B])

        cst = sb("cst", [128, C_END])
        ident = cst[:, C_IDENT:C_TRI]
        tri = cst[:, C_TRI:C_HEAD]
        headmask = cst[:, C_HEAD:C_RANK]
        rankrow = cst[:, C_RANK:C_SEG]
        segments = cst[:, C_SEG:C_TILE]
        tilestart = cst[0:1, C_TILE:C_ROW]
        ones = sb("ones", [128, 128])
        onesb = sb("onesb", [1, 128], BF16)
        zeros = sb("zeros", [128, PAIR])
        blank = sb("blank", [128, 4, D + 1])
        power = sb("power", [128, B])
        eps = sb("eps", [128, 1])
        gates = sb("gates", [128, 4])
        tg = sb("tg", [128, 4])
        wqT = sb("wqT", [128, D])
        wkT = sb("wkT", [128, D])
        wqk = sb("wqk", [128, D])
        cols = sb("cols", [128, 8])
        m0 = sb("m0", [128, 1])
        uq = sb("uq", [128, 1])
        c0 = sb("c0", [1, 1])
        wv01 = sb("wv01", [128, 2 * D])
        bv01 = sb("bv01", [SK, 2 * D])
        gain = sb("gain", [128, D])
        shift = sb("shift", [128, D])
        wk1 = sb("wk1", [128, D])
        wq1 = sb("wq1", [128, D])
        wo1 = sb("wo1", [128, D])
        bo1 = sb("bo1", [128, D])
        router = sb("router", [128, E])
        qscale = sb("qscale", [128, 1])
        qbias = sb("qbias", [128, 1])
        wgs = sb("wgs", [128, H])
        wus = sb("wus", [128, H])
        wds = sb("wds", [128, HC, D])
        wgu = sb("wgu", [128, E, 2 * H])
        wdn = sb("wdn", [128, E, HC * D])
        sgn = sb("sgn", [128, T])
        w2 = sb("w2", [128, T, D])
        b2 = sb("b2", [T, D])
        biasQ = sb("biasQ", [128, NH, SK])
        padR = sb("padR", [1, B, SK], BF16)
        nmax = sb("nmax", [128, B])
        slot = sb("slot", [128, B], U32)
        turn_experts = sb("turn_experts", [1, TURNS], I32)

        s_w = sem("s_w")
        s_late = sem("s_late")
        s_x = [sem(f"s_x{q}") for q in range(4)]
        s_zero = sem("s_zero")
        s_set = sem("s_set")
        s_pe0 = sem("s_pe0")
        s_act0 = sem("s_act0")
        s_dve0 = sem("s_dve0")
        s_pool0 = sem("s_pool0")
        s_stat = sem("s_stat")
        s_var = sem("s_var")
        s_window = sem("s_window")
        s_bias = sem("s_bias")
        padRi = sb("padRi", [1, B * SK], U8)

        row = lambda v: v.rearrange("(o n) -> o n", o=1)
        column = lambda v: v.rearrange("(n o) -> n o", o=1)

        early = [
            (wqT[:, :], a["wqT0"]), (wkT[:, :], a["wkT0"]),
            (cols[:, 0:1], column(a["bq0"])), (cols[:, 1:2], column(a["bk0"])),
            (cols[:, 2:3], column(a["bq1"])), (cols[:, 3:4], column(a["bk1"])),
            (cols[:, 4:5], column(a["logit_scale"])),
            (gates[:, 0:2], row(a["g_xattn"]).to_broadcast([128, 2])),
            (gates[:, 2:4], row(a["g_ffn"]).to_broadcast([128, 2])),
            (wv01[:, 0:D], a["wv0"]), (wv01[:, D:2 * D], a["wv1"]),
            (bv01[:, 0:D], row(a["bv0"]).to_broadcast([SK, D])),
            (bv01[:, D:2 * D], row(a["bv1"]).to_broadcast([SK, D])),
            (gain[:, :], row(a["gamma"]).to_broadcast([128, D])),
            (shift[:, :], row(a["beta"]).to_broadcast([128, D])),
            (wk1[:, :], a["wk1"]), (router[:, :], a["router"]), (cst[:, :], a["cst"]),
        ]
        late = [
            (bo1[:, :], row(a["bo1"]).to_broadcast([128, D])),
            (wq1[:, :], a["wq1"]), (wo1[:, :], a["wo1"]),
            (wgs[:, :], a["wgs"]), (wus[:, :], a["wus"]),
            (wds[:, :, :], a["wds"]),
            (padRi[:, :], row(a["pad"])),
            (sgn[:, :], a["sigs"]), (w2[:, :, :], a["w2"]), (b2[:, :], a["b2"]),
        ]
        n_late = len(late) + 2 * NG
        QB = B // 4

        with nc.Block() as block:
            @block.sync
            def _(sp):
                for q in range(4):
                    sp.dma_start(X[:, QB * q:QB * q + QB, :],
                                 a["x"][QB * q:QB * q + QB].rearrange("b s d -> s b d")).then_inc(s_x[q], 16)
                sp.wait_ge(s_w, 16 * len(early))
                sp.dma_start(wide_qk, bass.AP(tensor=a["table"].tensor, offset=128,
                                              ap=[[a["table"].shape[1], NH], [-1, 128], [1, SK]])).then_inc(s_window, 16)
                for dst, src in late:
                    sp.dma_start(dst, src).then_inc(s_late, 16)

            @block.gpsimd
            def _(pool):
                for q in range(4):
                    k = slice(QB * q, QB * q + QB)
                    pool.wait_ge(s_var, q + 1)
                    nc.gpsimd.tensor_tensor(rstd0[:, k], var0[:, k], power[:, 0:QB], ALU.pow).then_inc(s_pool0, 1)
                    pool.wait_ge(s_pool0, 2 * q + 1)
                    nc.gpsimd.tensor_tensor(nb0[:, k], nmean0[:, k], rstd0[:, k], ALU.mult).then_inc(s_pool0, 1)

            @block.scalar
            def _(act):
                for dst, src in early:
                    act.dma_start(dst, src).then_inc(s_w, 16)
                act.wait_ge(s_w, 16 * len(early))
                nc.scalar.activation(tg[:, :], gates[:, :], ACT.Tanh).then_inc(s_act0, 1)
                nc.scalar.activation(qscale[:, :], cols[:, 4:5], ACT.Exp).then_inc(s_act0, 1)
                act.wait_ge(s_pe0, 1)
                nc.scalar.activation(wqk[:, :], bank[0][:, 0:D], ACT.Copy).then_inc(s_act0, 1)
                nc.scalar.activation(m0[:, :], bank[0][:, D:D + 1], ACT.Copy, scale=D ** -0.5).then_inc(s_act0, 1)
                nc.scalar.activation(uq[:, :], bank[0][:, D + 1:D + 2], ACT.Copy).then_inc(s_act0, 1)
                nc.scalar.activation(c0[:, :], bank[0][0:1, D + 2:D + 3], ACT.Copy, scale=D ** -0.5).then_inc(s_act0, 1)

            @block.tensor
            def _(pe):
                pe.wait_ge(s_w, 16 * len(early))
                nc.tensor.matmul(bank[0][:, 0:D], wkT[:, :], wqT[:, :], start=True, stop=True)
                nc.tensor.matmul(bank[0][:, D:D + 1], wqT[:, :], cols[:, 1:2], start=True, stop=True)
                nc.tensor.matmul(bank[0][:, D + 1:D + 2], wkT[:, :], cols[:, 0:1], start=True, stop=True)
                nc.tensor.matmul(bank[0][0:1, D + 2:D + 3], cols[:, 0:1], cols[:, 1:2],
                                 start=True, stop=True).then_inc(s_pe0, 1)

            @block.vector
            def _(dve):
                nc.vector.memset(blank[:, :, :], 0.0).then_inc(s_set, 1)
                nc.vector.memset(zeros[:, :], 0.0)
                nc.vector.memset(ones[:, :], 1.0)
                nc.vector.memset(onesb[:, :], 1.0)
                nc.vector.memset(power[:, :], -0.5).then_inc(s_set, 1)
                nc.vector.memset(eps[:, :], EPS).then_inc(s_set, 1)
                step = [0]

                def then(ins):
                    step[0] += 1
                    ins.then_inc(s_stat, 1)
                    dve.wait_ge(s_stat, step[0])

                for q in range(4):
                    k = slice(QB * q, QB * q + QB)
                    var, mean = var0[:, k], nmean0[:, k]
                    me, mo = stats0[:, k, 1], stats0[:, k, 4]
                    dve.wait_ge(s_x[q], 16)
                    for b in range(QB * q, QB * q + QB):
                        last = nc.vector.bn_stats(stats0[:, b, :], X[:, b, :])
                    then(last)
                    then(nc.vector.tensor_tensor(var, me, mo, ALU.subtract))
                    then(nc.vector.scalar_tensor_tensor(out=var, in0=var, scalar=D / 4.0, in1=var,
                                                        op0=ALU.mult, op1=ALU.mult))
                    then(nc.vector.tensor_tensor(mean, stats0[:, k, 2], stats0[:, k, 5], ALU.add))
                    then(nc.vector.tensor_tensor(var, var, mean, ALU.add))
                    then(nc.vector.tensor_tensor(mean, me, mo, ALU.add))
                    then(nc.vector.tensor_scalar(mean, mean, -0.5, None, ALU.mult))
                    nc.vector.tensor_scalar(var, var, 1.0 / D, EPS, ALU.mult, ALU.add).then_inc(s_var, 1)
                dve.wait_ge(s_w, 16 * len(early))
                dve.wait_ge(s_set, 1)
                nc.vector.tensor_copy(blank[:, :, D], cst[:, C_SPARE:C_END])
                dve.wait_ge(s_act0, 2)
                for t in (gain, shift):
                    nc.vector.tensor_scalar(t[:, :], t[:, :], tg[:, 0:1], None, ALU.mult)
                nc.vector.tensor_scalar(qscale[:, :], qscale[:, :], 4.0, HD ** -0.5, ALU.min, ALU.mult).then_inc(s_dve0, 1)
                dve.wait_ge(s_dve0, 1)
                nc.vector.tensor_tensor(qbias[:, :], cols[:, 2:3], qscale[:, :], ALU.mult)
                rows = cst[:, C_ROW:C_SPARE].rearrange("p (b o) -> p b o", o=1)
                nc.vector.tensor_copy(XN[:, :, D:D + 1], rows).then_inc(s_dve0, 1)

        attend_0(nc, sem, sems, bank, a, locals())
        route(nc, sem, sems, bank, locals())
        experts(nc, sem, sems, bank, locals())
        attend_1(nc, sem, sems, bank, out, locals())


@phase
def attend_0(nc, sb, sem, sems, bank, a, m):
    X, XN, XNT, K1T, V1, LG = (m[k] for k in ("X", "XN", "XNT", "K1T", "V1", "LG"))
    nb0, rstd0, power, ident, ones, zeros = (m[k] for k in ("nb0", "rstd0", "power", "ident", "ones", "zeros"))
    wqk, m0, uq, c0, wk1, cols = (m[k] for k in ("wqk", "m0", "uq", "c0", "wk1", "cols"))
    wv01, bv01, gain, shift, router = (m[k] for k in ("wv01", "bv01", "gain", "shift", "router"))
    started, eps, nmax = m["s_set"], m["eps"], m["nmax"]
    two = range(2)
    PK = PAIR * SK
    ctxT = [sb(f"ctxT{u}", [128, PK]) for u in two]
    mask = [sb(f"mask{u}", [128, PAIR, SK], I32) for u in two]
    mbias = [sb(f"mbias{u}", [128, PAIR, SK]) for u in two]
    M = [sb(f"M{u}", [128, PK]) for u in two]
    crow = [sb(f"crow{u}", [1, PK]) for u in two]
    V0 = [sb(f"V0{u}", [SK, PAIR, D + 1]) for u in two]
    xn = [sb(f"xn{u}", [128, PAIR, D]) for u in two]
    xnT = [sb(f"xnT{u}", [128, PAIR, S]) for u in two]
    sm = [sb(f"sm{u}", [128, PAIR, SK]) for u in two]
    P = [sb(f"P{u}", [128, PAIR, SK]) for u in two]
    PT = [sb(f"PT{u}", [SK, PAIR, S]) for u in two]
    st = [sb(f"st{u}", [128, PAIR, 6]) for u in two]
    mv = [sb(f"mv{u}", [128, PAIR, 2]) for u in two]
    es = [sb(f"es{u}", [128, PAIR]) for u in two]
    vr = [sb(f"vr{u}", [128, PAIR]) for u in two]
    ru = [sb(f"ru{u}", [128, PAIR]) for u in two]
    t1 = [sb(f"t1{u}", [128, PAIR, D]) for u in two]
    xb = [sb(f"xb{u}", [128, PAIR, D]) for u in two]
    st1 = [sb(f"st1{u}", [128, PAIR, 6]) for u in two]
    mv1 = [sb(f"mv1{u}", [128, PAIR, 2]) for u in two]
    r1 = [sb(f"r1{u}", [128, PAIR]) for u in two]
    v1e = [sb(f"v1e{u}", [128, PAIR]) for u in two]
    xn1 = [sb(f"xn1{u}", [128, PAIR, D]) for u in two]
    xn1T = [sb(f"xn1T{u}", [128, PAIR, S]) for u in two]
    mr = [sb(f"mr{u}", [128, PAIR]) for u in two]
    nb1 = [sb(f"nb1{u}", [128, PAIR]) for u in two]

    bXT, bS, bPT, bU, bV, bMK, bT2, bLG = bank
    U = bU[:, 0:PAIR * (D + 1)].rearrange("p (b d) -> p b d", b=PAIR)
    s = sems("a", "set kv_v kv_m vev mev mb xn xT xnT sc sm mx ex pT pTs u ust umv ves vru t1 xb x1 "
                  "xst xmv vx r1 mr nb xn1 xn1c xT2 xT2s lg lgs uvr")
    l_ctx = [sem(f"a_ctx{u}") for u in two]
    l_mask = [sem(f"a_mask{u}") for u in two]

    with nc.Block() as block:
        @block.sync
        def _(sp):
            def load(g, u):
                wait(sp, s["kv_m"], g - 1)
                sp.dma_start(ctxT[u][:, :], a["ctxT"][:, bass.ds(g, 1), :].rearrange("p g k -> p (g k)")).then_inc(l_ctx[u], 16)
                wait(sp, s["mb"], g - 1)
                sp.dma_start(mask[u][:, :, :], a["mask"][:, bass.ds(PAIR * g, PAIR), :]).then_inc(l_mask[u], 16)

            def weights(g, u):
                for dst, src in ((m["wgu"], a["wgu"]), (m["wdn"], a["wdn"])):
                    parts = lambda v: v.rearrange("p e h -> p (e h)").rearrange("p (g h) -> p g h", g=NG)
                    sp.dma_start(parts(dst[:, :, :])[:, bass.ds(g, 1), :], parts(src)[:, bass.ds(g, 1), :]).then_inc(m["s_late"], 16)

            pipeline(sp, NG, [(load, 0), (weights, 0)])

        @block.tensor
        def _(pe):
            def norm_T(g, u):
                pe.wait_ge(s["xn"], g + 1)
                wait(pe, s["xnT"], g)
                for b in range(PAIR):
                    last = nc.tensor.transpose(bXT[:, b * 128:b * 128 + 128], xn[u][:, b, :], ident)
                last.then_inc(s["xT"], 1)

            def project(g, u):
                landed(pe, l_ctx, g, u)
                if isinstance(g, int) and g == 0:
                    pe.wait_ge(s["set"], 1)
                wait(pe, s["vev"], g)
                for b in range(PAIR):
                    last = nc.tensor.matmul(bV[0:SK, b * 2 * D:(b + 1) * 2 * D], ctxT[u][:, b * SK:(b + 1) * SK],
                                            wv01[:, :], start=True, stop=True)
                last.then_inc(s["kv_v"], 1)
                wait(pe, s["mev"], g)
                nc.tensor.matmul(bMK[:, 0:PK], wqk[:, :], ctxT[u][:, :], start=True, stop=True)
                nc.tensor.matmul(bMK[:, PK:2 * PK], wk1[:, :], ctxT[u][:, :], start=True, stop=True)
                nc.tensor.matmul(bMK[0:1, 2 * PK:3 * PK], uq[:, :], ctxT[u][:, :],
                                 start=True, stop=True).then_inc(s["kv_m"], 1)

            def scores(g, u):
                pe.wait_ge(s["xnT"], g + 1)
                pe.wait_ge(s["mev"], g + 1)
                wait(pe, s["sm"], g)
                for b in range(PAIR):
                    o = bS[:, b * SK:(b + 1) * SK]
                    nc.tensor.matmul(o, xnT[u][:, b, :], M[u][:, b * SK:(b + 1) * SK], start=True, stop=False)
                    last = nc.tensor.matmul(o, ones[0:1, :], crow[u][:, b * SK:(b + 1) * SK], start=False, stop=True)
                last.then_inc(s["sc"], 1)

            def probs_T(g, u):
                pe.wait_ge(s["ex"], g + 1)
                wait(pe, s["pTs"], g)
                for b in range(PAIR):
                    last = nc.tensor.transpose(bPT[0:SK, b * 128:b * 128 + 128], P[u][:, b, :], ident)
                last.then_inc(s["pT"], 1)

            def weigh(g, u):
                pe.wait_ge(s["pTs"], g + 1)
                pe.wait_ge(s["vev"], g + 1)
                wait(pe, s["t1"], g)
                for b in range(PAIR):
                    last = nc.tensor.matmul(U[:, b, :], PT[u][:, b, :], V0[u][:, b, :], start=True, stop=True)
                last.then_inc(s["u"], 1)

            def norm1_T(g, u):
                pe.wait_ge(s["xn1"], g + 1)
                wait(pe, s["xT2s"], g)
                for b in range(PAIR):
                    last = nc.tensor.transpose(bT2[:, b * 128:b * 128 + 128], xn1[u][:, b, :], ident)
                last.then_inc(s["xT2"], 1)

            def logits(g, u):
                pe.wait_ge(s["xT2s"], g + 1)
                wait(pe, s["lgs"], g)
                for b in range(PAIR):
                    last = nc.tensor.matmul(bLG[:, b * E:b * E + E], xn1T[u][:, b, :], router[:, :], start=True, stop=True)
                last.then_inc(s["lg"], 1)

            pipeline(pe, NG, [
                (project, 1), (norm_T, 0), (logits, 6), (probs_T, 2), (norm1_T, 5), (scores, 1), (weigh, 2)])

        @block.scalar
        def _(act):

            def exps(g, u):
                act.wait_ge(s["mx"], g + 1)
                wait(act, s["pT"], g - 1)
                for b in range(PAIR):
                    last = nc.scalar.activation(P[u][:, b, :], sm[u][:, b, :], ACT.Exp, bias=nmax[:, bass.ds(PAIR * g + b, 1)])
                last.then_inc(s["ex"], 1)

            def norm_T(g, u):
                act.wait_ge(s["xT"], g + 1)
                wait(act, s["sc"], g - 1)
                nc.scalar.activation(xnT[u][:, :, :].rearrange("p b s -> p (b s)"), bXT[:, 0:PAIR * S],
                                     ACT.Copy).then_inc(s["xnT"], 1)

            def probs_T(g, u):
                act.wait_ge(s["pT"], g + 1)
                wait(act, s["u"], g - 1)
                nc.scalar.activation(PT[u][:, :, :].rearrange("p b s -> p (b s)"), bPT[0:SK, 0:PAIR * S],
                                     ACT.Copy).then_inc(s["pTs"], 1)

            def keys(g, u):
                act.wait_ge(s["kv_m"], g + 1)
                wait(act, s["sc"], g - 1)
                nc.scalar.activation(M[u][:, :], bMK[:, 0:PK], ACT.Identity, bias=m0[:, 0:1], scale=D ** -0.5)
                nc.scalar.activation(K1T[:, bass.ds(PAIR * g, PAIR), :], bMK[:, PK:2 * PK].rearrange("p (b k) -> p b k", b=PAIR),
                                     ACT.Identity, bias=cols[:, 3:4])
                nc.scalar.activation(crow[u][:, :], bMK[0:1, 2 * PK:3 * PK], ACT.Identity, bias=c0[:, 0:1],
                                     scale=D ** -0.5).then_inc(s["mev"], 1)

            def norm1_T(g, u):
                act.wait_ge(s["xT2"], g + 1)
                wait(act, s["lg"], g - 1)
                src = bT2[:, 0:PAIR * S].rearrange("p (b s) -> p b s", b=PAIR)
                nc.scalar.activation(xn1T[u][:, :, :], src, ACT.Copy)
                nc.scalar.activation(XNT[:, bass.ds(PAIR * g, PAIR), :], src, ACT.Copy).then_inc(s["xT2s"], 1)

            def logits(g, u):
                act.wait_ge(s["lg"], g + 1)
                nc.scalar.activation(LG[:, bass.ds(PAIR * g, PAIR), :], bLG[:, 0:PAIR * E].rearrange("p (b e) -> p b e", b=PAIR),
                                     ACT.Copy).then_inc(s["lgs"], 1)

            def norm(g, u):
                wait(act, s["xT"], g - 1)
                for b in range(PAIR):
                    i = PAIR * g + b
                    last = nc.scalar.activation(xn[u][:, b:b + 1, :], X[:, bass.ds(i, 1), :], ACT.Identity,
                                                bias=nb0[:, bass.ds(i, 1)], scale=rstd0[:, bass.ds(i, 1)])
                last.then_inc(s["xn"], 1)

            def norm1(g, u):
                act.wait_ge(s["nb"], g + 1)
                wait(act, s["xT2"], g - 1)
                wait(act, s["xn1c"], g - 1)
                for b in range(PAIR):
                    last = nc.scalar.activation(xn1[u][:, b:b + 1, :], X[:, bass.ds(PAIR * g + b, 1), :], ACT.Identity,
                                                bias=nb1[u][:, b:b + 1], scale=r1[u][:, b:b + 1])
                last.then_inc(s["xn1"], 1)

            pipeline(act, NG, [
                (probs_T, 3), (logits, 7), (norm1_T, 6), (norm, 0), (exps, 2), (norm1, 5), (keys, 1),
                (norm_T, 0)])

        @block.vector
        def _(dve):
            for u in two:
                last = nc.vector.memset(V0[u][:, :, D:D + 1], 1.0)
            last.then_inc(s["set"], 1)

            def mask_bias(g, u):
                landed(dve, l_mask, g, u)
                wait(dve, s["sm"], g - 1)
                nc.vector.tensor_scalar(mbias[u][:, :, :], mask[u][:, :, :], 0.0, NEG, ALU.is_equal,
                                        ALU.mult).then_inc(s["mb"], 1)

            def masked(g, u):
                dve.wait_ge(s["sc"], g + 1)
                dve.wait_ge(s["mb"], g + 1)
                wait(dve, s["ex"], g - 1)
                flat = lambda t: t.rearrange("p b k -> p (b k)")
                nc.vector.tensor_tensor(flat(sm[u][:, :, :]), flat(mbias[u][:, :, :]), bS[:, 0:PK], ALU.add).then_inc(s["sm"], 1)
                dve.wait_ge(s["sm"], g + 1)
                nc.vector.tensor_reduce(nmax[:, bass.ds(PAIR * g, PAIR)], sm[u][:, :, :], AX.X, ALU.max, negate=True).then_inc(s["mx"], 1)

            def values(g, u):
                dve.wait_ge(s["kv_v"], g + 1)
                wait(dve, s["u"], g - 1)
                src = bV[0:SK, :].rearrange("p (b l d) -> p b l d", b=PAIR, l=2)
                bv = bv01[:, :].rearrange("p (l d) -> p l d", l=2)
                for layer, dst in ((0, V0[u][:, :, 0:D]), (1, V1[:, bass.ds(PAIR * g, PAIR), :])):
                    last = nc.vector.tensor_tensor(dst, src[:, :, layer, :],
                                                   bv[:, layer:layer + 1, :].to_broadcast([SK, PAIR, D]), ALU.add)
                last.then_inc(s["vev"], 1)

            def attend_stats(g, u):
                dve.wait_ge(s["u"], g + 1)
                wait(dve, s["vru"], g - 1)
                wait(dve, s["x1"], g - 1)
                for b in range(PAIR):
                    last = nc.vector.bn_stats(st[u][:, b, :], U[:, b, 0:D])
                last.then_inc(s["ust"], 1)
                nc.vector.tensor_scalar(es[u][:, :], U[:, :, D], EPS ** 0.5, None, ALU.mult)
                apart(dve, started)
                dve.wait_ge(s["ust"], g + 1)
                for b in range(PAIR):
                    last = nc.vector.bn_aggr(mv[u][:, b, :], st[u][:, b, :])
                last.then_inc(s["umv"], 1)
                dve.wait_ge(s["umv"], g + 1)
                for b in range(PAIR):
                    last = nc.vector.scalar_tensor_tensor(out=t1[u][:, b, :], in0=U[:, b, 0:D], scalar=mv[u][:, b, 0:1],
                                                          in1=gain[:, :], op0=ALU.subtract, op1=ALU.mult)
                last.then_inc(s["t1"], 1)

            def residual(g, u):
                dve.wait_ge(s["vru"], g + 1)
                dve.wait_ge(s["xb"], g + 1)
                dve.wait_ge(s["t1"], g + 1)
                wait(dve, s["nb"], g - 1)
                for b in range(PAIR):
                    last = nc.vector.scalar_tensor_tensor(out=X[:, bass.ds(PAIR * g + b, 1), :], in0=t1[u][:, b:b + 1, :],
                                                          scalar=ru[u][:, b:b + 1], in1=xb[u][:, b:b + 1, :],
                                                          op0=ALU.mult, op1=ALU.add)
                last.then_inc(s["x1"], 1)
                apart(dve, started)
                dve.wait_ge(s["x1"], g + 1)
                for b in range(PAIR):
                    last = nc.vector.bn_stats(st1[u][:, b, :], X[:, bass.ds(PAIR * g + b, 1), :])
                last.then_inc(s["xst"], 1)
                apart(dve, started)
                dve.wait_ge(s["xst"], g + 1)
                for b in range(PAIR):
                    last = nc.vector.bn_aggr(mv1[u][:, b, :], st1[u][:, b, :])
                last.then_inc(s["xmv"], 1)

            pipeline(dve, NG, [
                (values, 1), (residual, 3), (masked, 1), (attend_stats, 2), (mask_bias, 0)])

        @block.gpsimd
        def _(pool):

            def shifted(g, u):
                wait(pool, s["x1"], g - 1)
                nc.gpsimd.tensor_tensor(xb[u][:, :, :], X[:, bass.ds(PAIR * g, PAIR), :],
                                        shift[:, :].rearrange("p (o d) -> p o d", o=1).to_broadcast([128, PAIR, D]),
                                        ALU.add).then_inc(s["xb"], 1)

            def inv_std1(g, u):
                pool.wait_ge(s["xmv"], g + 1)
                wait(pool, s["xn1"], g - 1)
                nc.gpsimd.tensor_tensor(v1e[u][:, :], mv1[u][:, :, 1], eps[:, 0:1].to_broadcast([128, PAIR]), ALU.add).then_inc(s["vx"], 1)
                pool.wait_ge(s["vx"], g + 1)
                nc.gpsimd.tensor_tensor(r1[u][:, :], v1e[u][:, :], power[:, 0:PAIR], ALU.pow).then_inc(s["r1"], 1)
                pool.wait_ge(s["r1"], g + 1)
                nc.gpsimd.tensor_tensor(mr[u][:, :], mv1[u][:, :, 0], r1[u][:, :], ALU.mult).then_inc(s["mr"], 1)
                pool.wait_ge(s["mr"], g + 1)
                nc.gpsimd.tensor_tensor(nb1[u][:, :], zeros[:, 0:PAIR], mr[u][:, :], ALU.subtract).then_inc(s["nb"], 1)

            def keep(g, u):
                pool.wait_ge(s["xn1"], g + 1)
                nc.gpsimd.tensor_copy(XN[:, bass.ds(PAIR * g, PAIR), 0:D], xn1[u][:, :, :]).then_inc(s["xn1c"], 1)

            def inv_std0(g, u):
                pool.wait_ge(s["umv"], g + 1)
                wait(pool, s["x1"], g - 1)
                nc.gpsimd.tensor_tensor(vr[u][:, :], es[u][:, :], es[u][:, :], ALU.mult).then_inc(s["ves"], 1)
                pool.wait_ge(s["ves"], g + 1)
                nc.gpsimd.tensor_tensor(vr[u][:, :], vr[u][:, :], mv[u][:, :, 1], ALU.add).then_inc(s["uvr"], 1)
                pool.wait_ge(s["uvr"], g + 1)
                nc.gpsimd.tensor_tensor(ru[u][:, :], vr[u][:, :], power[:, 0:PAIR], ALU.pow).then_inc(s["vru"], 1)

            pipeline(pool, NG, [
                (keep, 4), (shifted, 0), (inv_std1, 2), (inv_std0, 1)])


@phase
def route(nc, sb, sem, sems, bank, m):
    X, XN, XNT, LG, ones, tri = (m[k] for k in ("X", "XN", "XNT", "LG", "ones", "tri"))
    wo1, bo1, wdn, w2, b2, tg, sgn = (m[k] for k in ("wo1", "bo1", "wdn", "w2", "b2", "tg", "sgn"))
    padR, padRi, s_late, n_late = (m[k] for k in ("padR", "padRi", "s_late", "n_late"))
    rankrow, segments, tilestart = (m[k] for k in ("rankrow", "segments", "tilestart"))
    slot, turn_experts, sorted_x = (m[k] for k in ("slot", "turn_experts", "sorted_x"))
    wgs, wus, wds = (m[k] for k in ("wgs", "wus", "wds"))
    best = sb("best", [128, B])
    cand = sb("cand", [128, B, E])
    OH = sb("OH", [128, B, E])
    counts = sb("counts", [128, E, B])
    upto = sb("upto", [128, E, B])
    padi = sb("padi", [128, E], I32)
    pad = sb("pad", [128, E])
    ends = sb("ends", [128, E])
    where = sb("where", [128, B, E])
    slotf = sb("slotf", [128, B])
    past = sb("past", [1, NTILE, E])
    tef = sb("tef", [1, DOWN + NTILE + DOWN])
    packed = sb("packed", [1, TURNS])
    sg = [sb(f"sg{c}", [128, 512]) for c in range(HC)]
    hT = [[sb(f"hT{u}{c}", [128, 512]) for c in range(HC)] for u in range(2)]
    s_r = sem("r_step")
    s_rank = sem("r_rank")
    s_gate = sem("r_gate")
    s_slot = sem("r_slot")
    s_scat = sem("r_scat")
    s = sems("f", "hid silu hT down add")
    NC = B * S // 512
    bank_of = [(bank[0], bank[1]), (bank[2], bank[3])]
    bRank, bCount = bank[6], bank[7]

    with nc.Block() as block:
        @block.sync
        def _(sp):
            for q in range(SLOTS // 512):
                sp.dma_start(sorted_x[512 * q:512 * q + 512].rearrange("(p r) d -> p (r d)", p=128),
                             m["blank"][:, :, :].rearrange("p r d -> p (r d)")).then_inc(m["s_zero"], 16)
            sp.wait_ge(m["s_window"], 16)
            sp.dma_start(m["biasQ"][:, :, :], m["wide_qk"].rearrange("h q k -> q h k")).then_inc(m["s_bias"], 16)

        @block.gpsimd
        def _(pool):
            pool.wait_ge(m["s_zero"], 16 * (SLOTS // 512))
            pool.wait_ge(s_slot, 1)
            for b in range(B):
                nc.gpsimd.indirect_dma_start(sorted_x, bass.IndirectOffsetOnAxis(ap=slot[:, b:b + 1], axis=0),
                                             XN[:, b, :], None).then_inc(s_scat, 16)
            pool.wait_ge(s_scat, 16 * B)

        @block.tensor
        def _(pe):
            pe.wait_ge(s_late, 16 * n_late)
            pe.wait_ge(s_gate, 1)
            flat = OH[:, :, :].rearrange("p b e -> p (b e)")

            def ranks():
                pe.wait_ge(s_r, 5)
                nc.tensor.matmul(bRank[:, 0:B * E], tri, flat, start=True, stop=True)
                nc.tensor.matmul(bCount[:, 0:B * E], ones[:, :], flat, start=True, stop=True).then_inc(s_rank, 1)

            def hidden(c, u):
                for k in range(HC):
                    gate, up = bank_of[k]
                    wait(pe, s["hT"], HC * (c - 1) + k + 1)
                    x = XNT[:, bass.ds(4 * c, 4), :]
                    nc.tensor.matmul(gate[:, :], wgs[:, k * 128:k * 128 + 128], x, start=True, stop=True)
                    nc.tensor.matmul(up[:, :], wus[:, k * 128:k * 128 + 128], x, start=True, stop=True).then_inc(s["hid"], 1)

            def down(c, u):
                pe.wait_ge(s["hT"], HC * c + HC)
                wait(pe, s["add"], c - 1)
                for t in range(4):
                    for k in range(HC):
                        last = nc.tensor.matmul(bank[4 + u][:, t * 128:t * 128 + 128], hT[u][k][:, t * 128:t * 128 + 128],
                                                wds[:, k, :], start=(k == 0), stop=(k == HC - 1))
                last.then_inc(s["down"], 1)

            ranks()
            pipeline(pe, NC, [(hidden, 0), (down, 1)])

        @block.scalar
        def _(act):
            def silu(c, u):
                for k in range(HC):
                    act.wait_ge(s["hid"], HC * c + k + 1)
                    wait(act, s["hT"], HC * (c - 1) + k + 1)
                    nc.scalar.activation(sg[k][:, :], bank_of[k][0][:, :], ACT.Silu).then_inc(s["silu"], 1)

            pipeline(act, NC, [(silu, 0)])
            act.wait_ge(s_late, 16 * n_late)
            nc.scalar.activation(sgn[:, :], sgn[:, :], ACT.Sign)

        @block.vector
        def _(dve):
            step = [0]

            def then(ins):
                step[0] += 1
                ins.then_inc(s_r, 1)
                dve.wait_ge(s_r, step[0])

            wide = lambda t: t.rearrange("p (b o) -> p b o", o=1).to_broadcast([128, B, E])
            dve.wait_ge(s_late, 16 * n_late)
            nc.vector.tensor_scalar(wds[:, :, :], wds[:, :, :], tg[:, 2:3], None, ALU.mult).then_inc(s_gate, 1)
            then(nc.vector.tensor_reduce(best[:, :], LG[:, :, :], AX.X, ALU.max))
            then(nc.vector.tensor_tensor(cand[:, :, :], LG[:, :, :], wide(best[:, :]), ALU.is_equal))
            then(nc.vector.tensor_tensor(cand[:, :, :], cand[:, :, :],
                                         rankrow.rearrange("p (o e) -> p o e", o=1).to_broadcast([128, B, E]), ALU.mult))
            then(nc.vector.tensor_reduce(best[:, :], cand[:, :, :], AX.X, ALU.max))
            then(nc.vector.tensor_tensor(OH[:, :, :], cand[:, :, :], wide(best[:, :]), ALU.is_equal))
            dve.wait_ge(s_rank, 1)
            then(nc.vector.tensor_copy(counts[:, :, :], bCount[:, 0:B * E].rearrange("p (b e) -> p e b", e=E)))
            then(nc.vector.tensor_tensor_scan(upto[:, :, :].rearrange("p e b -> p (e b)"), segments,
                                              counts[:, :, :].rearrange("p e b -> p (e b)"), 0.0, ALU.mult, ALU.add))
            then(nc.vector.tensor_scalar(padi[:, :], upto[:, :, B - 1], 127.0, None, ALU.add))
            then(nc.vector.tensor_scalar(padi[:, :], padi[:, :], 7, 7, ALU.arith_shift_right, ALU.logical_shift_left))
            then(nc.vector.tensor_copy(pad[:, :], padi[:, :]))
            then(nc.vector.tensor_tensor_scan(ends[:, :], ones[:, 0:E], pad[:, :], 0.0, ALU.mult, ALU.add))
            then(nc.vector.tensor_tensor(pad[:, :], ends[:, :], pad[:, :], ALU.subtract))
            then(nc.vector.tensor_tensor(upto[:, :, :], upto[:, :, :], counts[:, :, :], ALU.subtract))
            then(nc.vector.tensor_tensor(upto[:, :, :], upto[:, :, :],
                                         pad[:, :].rearrange("p (e o) -> p e o", o=1).to_broadcast([128, E, B]), ALU.add))
            then(nc.vector.tensor_tensor(where[:, :, :], bRank[:, 0:B * E].rearrange("p (b e) -> p b e", e=E),
                                         upto[:, :, :].rearrange("p e b -> p b e"), ALU.add))
            then(nc.vector.tensor_tensor(where[:, :, :], where[:, :, :], OH[:, :, :], ALU.mult))
            then(nc.vector.tensor_reduce(slotf[:, :], where[:, :, :], AX.X, ALU.add))
            nc.vector.tensor_copy(slot[:, :], slotf[:, :]).then_inc(s_slot, 1)
            then(nc.vector.tensor_tensor(past[:, :, :], tilestart.rearrange("p (t o) -> p t o", o=1).to_broadcast([1, NTILE, E]),
                                         ends[0:1, :].rearrange("p (o e) -> p o e", o=1).to_broadcast([1, NTILE, E]), ALU.is_ge))
            then(nc.vector.memset(tef[:, :], 0.0))
            own = tef[:, DOWN:DOWN + NTILE]
            then(nc.vector.tensor_reduce(own, past[:, :, :], AX.X, ALU.add))
            then(nc.vector.tensor_scalar(own, own, float(E - 1), None, ALU.min))
            every = lambda first: tef[:, DOWN + first:DOWN + first + 2 * TURNS].rearrange("p (i u) -> p i u", u=2)[:, :, 0]
            then(nc.vector.tensor_copy(packed[:, :], every(1 - DOWN)))
            for first in (-DOWN, 1 - UP):
                then(nc.vector.scalar_tensor_tensor(out=packed[:, :], in0=packed[:, :], scalar=float(E), in1=every(first),
                                                    op0=ALU.mult, op1=ALU.add))
            then(nc.vector.scalar_tensor_tensor(out=turn_experts[:, :], in0=packed[:, :], scalar=float(E), in1=every(-UP),
                                                op0=ALU.mult, op1=ALU.add))

            def product(c, u):
                for k in range(HC):
                    dve.wait_ge(s["silu"], HC * c + k + 1)
                    wait(dve, s["down"], c - 1)
                    nc.vector.tensor_tensor(hT[u][k][:, :], sg[k][:, :], bank_of[k][1][:, :], ALU.mult).then_inc(s["hT"], 1)

            def add(c, u):
                dve.wait_ge(s["down"], c + 1)
                x = X[:, bass.ds(4 * c, 4), :]
                nc.vector.tensor_tensor(x, x, bank[4 + u][:, :].rearrange("p (b d) -> p b d", b=4), ALU.add).then_inc(s["add"], 1)

            pipeline(dve, NC, [(product, 0), (add, 1)])
            for t, g in ((wo1, 1), (bo1, 1), (wdn, 2), (w2, 3)):
                nc.vector.tensor_scalar(t[:], t[:], tg[:, g:g + 1], None, ALU.mult)
            nc.vector.tensor_scalar(b2[:, :], b2[:, :], tg[0:T, 3:4], None, ALU.mult)
            dve.wait_ge(m["s_bias"], 16)
            nc.vector.tensor_scalar(padR[:, :, :].rearrange("p b k -> p (b k)"), padRi[:, :], PADDED, None, ALU.mult)


@phase
def experts(nc, sb, sem, sems, bank, m):
    ident, turn_experts, sorted_x, routed = (m[k] for k in ("ident", "turn_experts", "sorted_x", "routed"))
    wgu, wdn = m["wgu"], m["wdn"]
    two, WAYS = range(2), 4
    xs = [sb(f"xs{u}", [128, D]) for u in two]
    targets = sb("targets", [128, NTILE])
    targets_i = sb("targets_i", [128, NTILE], U32)
    izero = sb("izero", [128, 1], U32)
    to = [sb(f"to{w}", [128, 1], U32) for w in range(WAYS)]
    xsT = [sb(f"xsT{u}", [128, 128]) for u in two]
    act_g = [sb(f"actg{u}", [128, H]) for u in two]
    hid = [sb(f"hid{u}", [128, H]) for u in two]
    hidT = [sb(f"hidT{u}", [128, HC, 128]) for u in two]
    ys = [sb(f"ys{w}", [128, D]) for w in range(WAYS)]
    l_x = [sem(f"e_x{u}") for u in two]
    l_targets = sem("e_targets")
    st_y = [sem(f"e_y{w}") for w in range(WAYS)]
    s = sems("e", "set to xT xTs h silu hid hT hTs y ys")
    bX, bH, bHT, bY = bank[0:2], bank[2:4], bank[4:6], bank[6:8]
    rows = lambda t, i, k: t.rearrange("(t p) d -> t p d", p=128)[bass.ds(i, 1), :, k].rearrange("o p d -> (o p) d")

    with nc.Block() as block:
        @block.sync
        def _(sp):
            def load(t, u):
                wait(sp, s["xT"], t - 1)
                sp.dma_start(xs[u][:, :], rows(sorted_x, t, slice(0, D))).then_inc(l_x[u], 16)

            pipeline(sp, NTILE, [(load, 0)])

        @block.gpsimd
        def _(pool):
            def store(t, w):
                pool.wait_ge(s["ys"], t + 1)
                free(pool, st_y, t, w)
                nc.gpsimd.tensor_tensor(to[w][:, :], targets_i[:, bass.ds(t, 1)], izero[:, :], ALU.add).then_inc(s["to"], 1)
                apart(pool, m["s_set"])
                pool.wait_ge(s["to"], t + 1)
                nc.gpsimd.indirect_dma_start(routed, bass.IndirectOffsetOnAxis(ap=to[w][:, 0:1], axis=0),
                                             ys[w][:, :], None).then_inc(st_y[w], 16)

            pool.wait_ge(s["set"], 2)
            pipeline(pool, NTILE, [(store, 0)], WAYS)
            for w in range(WAYS):
                pool.wait_ge(st_y[w], 16 * NTILE // WAYS)

        @block.tensor
        def _(pe):
            def rows_T(t, u):
                landed(pe, l_x, t, u)
                wait(pe, s["xTs"], t - 1)
                nc.tensor.transpose(bX[u][:, 0:128], xs[u][:, :], ident).then_inc(s["xT"], 1)

            now = [None]

            def lookup(i):
                now[0] = nc.tensor.value_load(turn_experts[0:1, bass.ds(i, 1)], min_val=0, max_val=E ** 4 - 1)

            def expert(place):
                return ((now[0] >> (3 * place)) & (E - 1)).with_bounds(min_val=0, max_val=E - 1)

            def up(t, u):
                pe.wait_ge(s["xTs"], t + 1)
                wait(pe, s["hid"], t - 1)
                e = expert((u + UP) % 2)
                nc.tensor.matmul(bH[u][:, :], xsT[u][:, :], wgu[:, bass.ds(e, 1), :], start=True, stop=True).then_inc(s["h"], 1)

            def hidden_T(t, u):
                pe.wait_ge(s["hid"], t + 1)
                wait(pe, s["hTs"], t - 1)
                for k in range(HC):
                    last = nc.tensor.transpose(bHT[u][:, k * 128:k * 128 + 128], hid[u][:, k * 128:k * 128 + 128], ident)
                last.then_inc(s["hT"], 1)

            def down(t, u):
                pe.wait_ge(s["hTs"], t + 1)
                wait(pe, s["ys"], t - 1)
                e = expert(2 + (u + DOWN) % 2)
                for k in range(HC):
                    last = nc.tensor.matmul(bY[u][:, 0:D], hidT[u][:, k, :], wdn[:, bass.ds(e, 1), k * D:(k + 1) * D],
                                            start=(k == 0), stop=(k == HC - 1))
                last.then_inc(s["y"], 1)

            pipeline(pe, NTILE, [
                (down, DOWN), (rows_T, 0), (hidden_T, 3), (up, UP)], begin=lookup)

        @block.scalar
        def _(act):
            with nc.allow_non_contiguous_dma(reason="one number of each row"):
                act.dma_start(targets[:, :], sorted_x.rearrange("(t p) d -> p t d", p=128)[:, :, D]).then_inc(l_targets, 16)

            def rows_T(t, u):
                act.wait_ge(s["xT"], t + 1)
                wait(act, s["h"], t - 1)
                nc.scalar.activation(xsT[u][:, :], bX[u][:, 0:128], ACT.Copy).then_inc(s["xTs"], 1)

            def silu(t, u):
                act.wait_ge(s["h"], t + 1)
                wait(act, s["hid"], t - 1)
                nc.scalar.activation(act_g[u][:, :], bH[u][:, 0:H], ACT.Silu).then_inc(s["silu"], 1)

            def hidden_T(t, u):
                act.wait_ge(s["hT"], t + 1)
                wait(act, s["y"], t - 1)
                nc.scalar.activation(hidT[u][:, :, :].rearrange("p k t -> p (k t)"), bHT[u][:, 0:H], ACT.Copy).then_inc(s["hTs"], 1)

            pipeline(act, NTILE, [(rows_T, 0), (hidden_T, 3), (silu, 1)])

        @block.vector
        def _(dve):
            def product(t, w):
                u = w % 2
                dve.wait_ge(s["silu"], t + 1)
                wait(dve, s["hT"], t - 1)
                nc.vector.tensor_tensor(hid[u][:, :], act_g[u][:, :], bH[u][:, H:2 * H], ALU.mult).then_inc(s["hid"], 1)

            nc.vector.memset(izero[:, :], 0).then_inc(s["set"], 1)
            dve.wait_ge(l_targets, 16)
            nc.vector.tensor_copy(targets_i[:, :], targets[:, :]).then_inc(s["set"], 1)

            def result(t, w):
                u = w % 2
                dve.wait_ge(s["y"], t + 1)
                free(dve, st_y, t, w)
                nc.vector.tensor_copy(ys[w][:, :], bY[u][:, 0:D]).then_inc(s["ys"], 1)

            pipeline(dve, NTILE, [(result, 2), (product, 0)], WAYS)


@phase
def attend_1(nc, sb, sem, sems, bank, out, m):
    X, K1T, V1, power, ident = (m[k] for k in ("X", "K1T", "V1", "power", "ident"))
    headmask, biasQ, padR, onesb, routed = (m[k] for k in ("headmask", "biasQ", "padR", "onesb", "routed"))
    wq1, qscale, qbias, wo1, bo1 = (m[k] for k in ("wq1", "qscale", "qbias", "wo1", "bo1"))
    sgn, w2, b2, rankrow = (m[k] for k in ("sgn", "w2", "b2", "rankrow"))
    started, eps = m["s_set"], m["eps"]
    two = range(2)
    x2 = [sb(f"x2{u}", [128, D]) for u in two]
    x2b = [sb(f"x2b{u}", [128, D]) for u in two]
    st2 = [sb(f"st2{u}", [128, 6]) for u in two]
    mv2 = [sb(f"mv2{u}", [128, 2]) for u in two]
    v2e = [sb(f"v2e{u}", [128, 1]) for u in two]
    r2 = [sb(f"r2{u}", [128, 1]) for u in two]
    xn2 = [sb(f"xn2{u}", [128, D]) for u in two]
    xn2T = [sb(f"xn2T{u}", [128, S]) for u in two]
    QT = [sb(f"QT{u}", [128, S]) for u in two]
    KB = [sb(f"KB{u}", [128, NH, SK]) for u in two]
    VP = [sb(f"VP{u}", [SK, NH, 32]) for u in two]
    nmax, dead = m["nmax"], sb("dead", [128, B])
    y = [sb(f"y{u}", [128, D]) for u in two]
    SC = [sb(f"SC{u}", [128, NH, SK]) for u in two]
    top = [sb(f"top{u}", [128, NH]) for u in two]
    P = [sb(f"PR{u}", [128, NH, SK]) for u in two]
    PT = [sb(f"PRT{u}", [SK, HG * S]) for u in two]
    OS = [sb(f"OS{u}", [128, NCH, S]) for u in two]
    rden = [sb(f"rden{u}", [128, NCH, HG]) for u in two]
    AO = [sb(f"AO{u}", [128, D]) for u in two]
    AOT = [sb(f"AOT{u}", [128, S]) for u in two]
    x3 = [sb(f"x3{u}", [128, D]) for u in two]
    st3 = [sb(f"st3{u}", [128, 6]) for u in two]
    mv3 = [sb(f"mv3{u}", [128, 2]) for u in two]
    v3e = [sb(f"v3e{u}", [128, 1]) for u in two]
    r3 = [sb(f"r3{u}", [128, 1]) for u in two]
    xn3 = [sb(f"xn3{u}", [128, D]) for u in two]
    xn3T = [sb(f"xn3T{u}", [128, S]) for u in two]
    am = [sb(f"am{u}", [128, 4, T]) for u in two]
    OH = [sb(f"OH{u}", [128, T]) for u in two]
    OHT = [sb(f"OHT{u}", [T, S]) for u in two]
    picked = [sb(f"picked{u}", [128, T, D]) for u in two]
    sum4 = [sb(f"sum4{u}", [128, 4, D]) for u in two]
    x3b = [sb(f"x3b{u}", [128, D]) for u in two]
    res = [sb(f"res{u}", [128, D]) for u in two]

    bS, bP, bO, bA, bB, bF = bank[0:2], bank[2:4], bank[4], bank[5], bank[6], bank[7]
    HT = T // 2
    NHF = 2
    HH = NH // NHF
    s = sems("d", "set clear x2 x2b st2 mv2 v2 r2 xn2 xT xTs q qs kb vp sc sb mx su ex pT pTs pv os oT "
                  "rd ao aT aTs y x3 st3 mv3 v3 r3 xn3 zT zTs sg am oh hT hTs f pk fb x3b s4 s2 s1 res")
    st_o = [sem(f"d_out{u}") for u in two]
    l_y = [sem(f"d_y{u}") for u in two]
    N = NCH

    with nc.Block() as block:
        @block.tensor
        def _(pe):
            pe.wait_ge(s["set"], 1)

            def norm_T(b, u):
                pe.wait_ge(s["xn2"], b + 1)
                wait(pe, s["qs"], b)
                nc.tensor.transpose(bA[:, 0:128], xn2[u][:, :], ident).then_inc(s["xT"], 1)

            def queries(b, u):
                pe.wait_ge(s["xTs"], b + 1)
                nc.tensor.matmul(bA[:, 0:128], wq1[:, :], xn2T[u][:, :], start=True, stop=True).then_inc(s["q"], 1)

            def scores(c):
                def stage(b, u):
                    if c == 0:
                        pe.wait_ge(s["qs"], b + 1)
                        pe.wait_ge(s["kb"], b + 1)
                    wait(pe, s["sb"], N * b + c - 1)
                    o = bS[c % 2][:, 0:HG * SK]
                    nc.tensor.matmul(o, QT[u][:, :], KB[u][:, c * HG:(c + 1) * HG, :], start=True, stop=False)
                    nc.tensor.matmul(o, onesb[:, :], padR[:, bass.ds(b, 1), :].to_broadcast([1, HG, SK]),
                                     start=False, stop=True).then_inc(s["sc"], 1)
                return stage

            def probs_T(c):
                def stage(b, u):
                    pe.wait_ge(s["ex"], NHF * b + c * HG // HH + 1)
                    wait(pe, s["pTs"], N * b + c - 1)
                    for j in range(HG):
                        last = nc.tensor.transpose(bP[c % 2][0:SK, j * 128:j * 128 + 128], P[u][:, c * HG + j, :], ident)
                    last.then_inc(s["pT"], 1)
                return stage

            def weigh(c):
                def stage(b, u):
                    pe.wait_ge(s["pTs"], N * b + c + 1)
                    if c == 0:
                        pe.wait_ge(s["vp"], b + 1)
                        wait(pe, s["os"], b)
                    for j in range(HG):
                        last = nc.tensor.matmul(bO[32 * j:32 * j + 32, c * 128:c * 128 + 128], VP[u][:, c * HG + j, :],
                                                PT[c % 2][:, j * 128:j * 128 + 128], start=True, stop=True)
                    last.then_inc(s["pv"], 1)
                return stage

            def heads_T(b, u):
                pe.wait_ge(s["os"], b + 1)
                wait(pe, s["x3"], b)
                for c in range(NCH):
                    last = nc.tensor.transpose(bB[:, c * 128:c * 128 + 128], OS[u][:, c, :], ident)
                last.then_inc(s["oT"], 1)

            def mixed_T(b, u):
                pe.wait_ge(s["ao"], b + 1)
                nc.tensor.transpose(bB[:, 0:128], AO[u][:, :], ident).then_inc(s["aT"], 1)

            def project(b, u):
                pe.wait_ge(s["aTs"], b + 1)
                nc.tensor.matmul(bB[:, 0:128], AOT[u][:, :], wo1[:, :], start=True, stop=True).then_inc(s["y"], 1)

            def norm3_T(b, u):
                pe.wait_ge(s["xn3"], b + 1)
                wait(pe, s["x3b"], b)
                nc.tensor.transpose(bF[:, 0:128], xn3[u][:, :], ident).then_inc(s["zT"], 1)

            def signature(b, u):
                pe.wait_ge(s["zTs"], b + 1)
                nc.tensor.matmul(bF[:, 0:T], xn3T[u][:, :], sgn[:, :], start=True, stop=True).then_inc(s["sg"], 1)

            def maps(k):
                def stage(b, u):
                    if k == 0:
                        pe.wait_ge(s["hTs"], b + 1)
                    else:
                        pe.wait_ge(s["pk"], 2 * b + 1)
                    nc.tensor.matmul(bF[:, :], xn3T[u][:, :], w2[:, k * HT:(k + 1) * HT, :], start=True, stop=True).then_inc(s["f"], 1)
                return stage

            def choice_T(b, u):
                pe.wait_ge(s["oh"], b + 1)
                nc.tensor.transpose(bF[0:T, 0:128], OH[u][:, :], ident).then_inc(s["hT"], 1)

            def picked_bias(b, u):
                pe.wait_ge(s["pk"], 2 * b + 2)
                nc.tensor.matmul(bF[:, 0:128], OHT[u][:, :], b2[:, :], start=True, stop=True).then_inc(s["fb"], 1)

            pipeline(pe, B, [
                (probs_T(0), 2), (maps(1), 4), (mixed_T, 3), (scores(0), 1), (project, 3), (probs_T(1), 2),
                (picked_bias, 4), (scores(1), 1), (probs_T(2), 2), (probs_T(3), 2), (weigh(0), 2),
                (norm3_T, 3), (weigh(1), 2), (signature, 3), (scores(2), 1), (weigh(2), 2), (choice_T, 3),
                (scores(3), 1), (weigh(3), 2), (maps(0), 3), (norm_T, 0), (heads_T, 2), (queries, 0)])

        @block.scalar
        def _(act):

            def norm_T(b, u):
                act.wait_ge(s["xT"], b + 1)
                wait(act, s["q"], b - 1)
                nc.scalar.activation(xn2T[u][:, :], bA[:, 0:128], ACT.Copy).then_inc(s["xTs"], 1)

            def queries(b, u):
                act.wait_ge(s["q"], b + 1)
                wait(act, s["sc"], N * (b - 1))
                nc.scalar.activation(QT[u][:, :], bA[:, 0:128], ACT.Identity, bias=qbias[:, 0:1],
                                     scale=qscale[:, 0:1]).then_inc(s["qs"], 1)

            def exps(h):
                def stage(b, u):
                    act.wait_ge(s["su"], NHF * b + h + 1)
                    if h == 0:
                        wait(act, s["pT"], N * (b - 1))
                    k = slice(h * HH, (h + 1) * HH)
                    nc.scalar.activation(P[u][:, k, :], SC[u][:, k, :], ACT.Exp).then_inc(s["ex"], 1)
                return stage

            def probs_T(c):
                def stage(b, u):
                    act.wait_ge(s["pT"], N * b + c + 1)
                    wait(act, s["pv"], N * b + c - 1)
                    nc.scalar.activation(PT[c % 2][:, :], bP[c % 2][0:SK, :], ACT.Copy).then_inc(s["pTs"], 1)
                return stage

            def heads(b, u):
                act.wait_ge(s["pv"], N * (b + 1))
                wait(act, s["oT"], b - 1)
                nc.scalar.activation(OS[u][:, :, :].rearrange("p c s -> p (c s)"), bO[:, :], ACT.Copy).then_inc(s["os"], 1)

            def mixed_T(b, u):
                act.wait_ge(s["aT"], b + 1)
                wait(act, s["y"], b - 1)
                nc.scalar.activation(AOT[u][:, :], bB[:, 0:128], ACT.Copy).then_inc(s["aTs"], 1)

            def norm3_T(b, u):
                act.wait_ge(s["zT"], b + 1)
                wait(act, s["f"], 2 * (b - 1))
                nc.scalar.activation(xn3T[u][:, :], bF[:, 0:128], ACT.Copy).then_inc(s["zTs"], 1)

            def choice_T(b, u):
                act.wait_ge(s["hT"], b + 1)
                wait(act, s["fb"], b - 1)
                nc.scalar.activation(OHT[u][:, :], bF[0:T, 0:128], ACT.Copy).then_inc(s["hTs"], 1)

            pipeline(act, B, [
                (norm3_T, 3), (probs_T(2), 2), (probs_T(3), 2), (choice_T, 3), (exps(0), 1), (heads, 2),
                (norm_T, 0), (queries, 0), (mixed_T, 2), (probs_T(0), 1), (exps(1), 1), (probs_T(1), 1)])

        @block.vector
        def _(dve):
            for u in two:
                nc.vector.memset(VP[u][:, :, :], 0.0).then_inc(s["clear"], 1)
            dve.wait_ge(s["clear"], 2)
            for u in two:
                last = nc.vector.memset(VP[u][:, :, HD:HD + 1], 1.0)
            last.then_inc(s["set"], 1)
            nc.vector.tensor_scalar(dead[:, :], nmax[:, :], 4.0, 0.0, ALU.mult, ALU.mult).then_inc(s["clear"], 1)
            dve.wait_ge(s["clear"], 3)

            def stats2(b, u):
                apart(dve, started)
                dve.wait_ge(s["x2"], b + 1)
                wait(dve, s["r2"], b - 1)
                nc.vector.bn_stats(st2[u][:, :], x2[u][:, :]).then_inc(s["st2"], 1)
                apart(dve, started)
                dve.wait_ge(s["st2"], b + 1)
                nc.vector.bn_aggr(mv2[u][:, :], st2[u][:, :]).then_inc(s["mv2"], 1)

            def norm2(b, u):
                dve.wait_ge(s["r2"], b + 1)
                dve.wait_ge(s["mv2"], b + 1)
                wait(dve, s["xT"], b - 1)
                nc.vector.tensor_scalar(xn2[u][:, :], x2[u][:, :], mv2[u][:, 0:1], r2[u][:, 0:1],
                                        ALU.subtract, ALU.mult).then_inc(s["xn2"], 1)

            def bias(c):
                def stage(b, u):
                    dve.wait_ge(s["sc"], N * b + c + 1)
                    if c == 0:
                        wait(dve, s["ex"], NHF * (b - 1))
                    k = slice(c * HG, (c + 1) * HG)
                    nc.vector.tensor_tensor(SC[u][:, k, :], bS[c % 2][:, 0:HG * SK].rearrange("p (h k) -> p h k", h=HG),
                                            biasQ[:, k, :], ALU.add).then_inc(s["sb"], 1)
                return stage

            def maxima(h):
                def stage(b, u):
                    dve.wait_ge(s["sb"], N * b + (h + 1) * N // NHF)
                    k = slice(h * HH, (h + 1) * HH)
                    nc.vector.tensor_reduce(top[u][:, k], SC[u][:, k, :], AX.X, ALU.max).then_inc(s["mx"], 1)
                return stage

            def subtract(h):
                def stage(b, u):
                    dve.wait_ge(s["mx"], NHF * b + h + 1)
                    k = slice(h * HH, (h + 1) * HH)
                    nc.vector.tensor_tensor(SC[u][:, k, :], SC[u][:, k, :],
                                            top[u][:, k].rearrange("p (h o) -> p h o", o=1).to_broadcast([128, HH, SK]),
                                            ALU.subtract).then_inc(s["su"], 1)
                return stage

            def mix(b, u):
                dve.wait_ge(s["oT"], b + 1)
                wait(dve, s["aT"], b - 1)
                v = bB[:, :].rearrange("p (c j r) -> p c j r", c=NCH, j=HG)
                nc.vector.reciprocal(rden[u][:, :, :], v[:, :, :, HD]).then_inc(s["rd"], 1)
                dve.wait_ge(s["rd"], b + 1)
                nc.vector.tensor_tensor(AO[u][:, :].rearrange("p (c j r) -> p c j r", c=NCH, j=HG), v[:, :, :, 0:HD],
                                        rden[u][:, :, :].rearrange("p c (j o) -> p c j o", o=1).to_broadcast([128, NCH, HG, HD]),
                                        ALU.mult).then_inc(s["ao"], 1)

            def residual(b, u):
                dve.wait_ge(s["y"], b + 1)
                dve.wait_ge(s["x2b"], b + 1)
                wait(dve, s["x3b"], b - 1)
                wait(dve, s["r3"], b - 1)
                nc.vector.tensor_tensor(x3[u][:, :], bB[:, 0:128], x2b[u][:, :], ALU.add).then_inc(s["x3"], 1)
                dve.wait_ge(s["x3"], b + 1)
                nc.vector.bn_stats(st3[u][:, :], x3[u][:, :]).then_inc(s["st3"], 1)
                apart(dve, started)
                dve.wait_ge(s["st3"], b + 1)
                nc.vector.bn_aggr(mv3[u][:, :], st3[u][:, :]).then_inc(s["mv3"], 1)

            def norm3(b, u):
                dve.wait_ge(s["r3"], b + 1)
                dve.wait_ge(s["mv3"], b + 1)
                wait(dve, s["zT"], b - 1)
                nc.vector.tensor_scalar(xn3[u][:, :], x3[u][:, :], mv3[u][:, 0:1], r3[u][:, 0:1],
                                        ALU.subtract, ALU.mult).then_inc(s["xn3"], 1)

            def choose(b, u):
                dve.wait_ge(s["sg"], b + 1)
                wait(dve, s["hT"], b - 1)
                t = am[u]
                n = 3 * b
                nc.vector.tensor_reduce(t[:, 0, 0:1], bF[:, 0:T], AX.X, ALU.max).then_inc(s["am"], 1)
                dve.wait_ge(s["am"], n + 1)
                nc.vector.scalar_tensor_tensor(out=t[:, 1, :], in0=bF[:, 0:T], scalar=t[:, 0, 0:1], in1=rankrow,
                                               op0=ALU.is_equal, op1=ALU.mult).then_inc(s["am"], 1)
                dve.wait_ge(s["am"], n + 2)
                nc.vector.tensor_reduce(t[:, 2, 0:1], t[:, 1, :], AX.X, ALU.max).then_inc(s["am"], 1)
                dve.wait_ge(s["am"], n + 3)
                nc.vector.tensor_scalar(OH[u][:, :], t[:, 1, :], t[:, 2, 0:1], None, ALU.is_equal).then_inc(s["oh"], 1)

            def pick(k):
                def stage(b, u):
                    dve.wait_ge(s["f"], 2 * b + k + 1)
                    dve.wait_ge(s["oh"], b + 1)
                    wait(dve, s["s4"], b - 1)
                    nc.vector.tensor_tensor(picked[u][:, k * HT:(k + 1) * HT, :],
                                            bF[:, :].rearrange("p (t d) -> p t d", t=HT),
                                            OH[u][:, k * HT:(k + 1) * HT].rearrange("p (t o) -> p t o", o=1).to_broadcast([128, HT, D]),
                                            ALU.mult).then_inc(s["pk"], 1)
                return stage

            def add_bias(b, u):
                dve.wait_ge(s["fb"], b + 1)
                wait(dve, s["res"], b - 1)
                nc.vector.scalar_tensor_tensor(out=x3b[u][:, :], in0=bF[:, 0:128], scalar=dead[:, bass.ds(b, 1)],
                                               in1=x3[u][:, :], op0=ALU.add, op1=ALU.add).then_inc(s["x3b"], 1)

            pipeline(dve, B, [
                (mix, 3), (subtract(1), 2), (stats2, 0), (pick(1), 4), (residual, 3), (bias(0), 1),
                (add_bias, 4), (bias(1), 1), (norm3, 3), (maxima(0), 1), (choose, 3), (subtract(0), 1),
                (norm2, 0), (bias(2), 1), (bias(3), 1), (maxima(1), 1), (pick(0), 3)])

        @block.gpsimd
        def _(pool):
            pool.wait_ge(s["set"], 1)
            def keys(b, u):
                wait(pool, s["sc"], N * (b - 1))
                nc.gpsimd.tensor_tensor(KB[u][:, :, :], K1T[:, bass.ds(b, 1), :].to_broadcast([128, NH, SK]),
                                        headmask.rearrange("p (h o) -> p h o", o=1).to_broadcast([128, NH, SK]),
                                        ALU.mult).then_inc(s["kb"], 1)

            def values(b, u):
                wait(pool, s["pv"], N * (b - 1))
                nc.gpsimd.tensor_copy(VP[u][:, :, 0:HD],
                                      V1[:, bass.ds(b, 1), :].rearrange("k o (h d) -> k (o h) d", h=NH)).then_inc(s["vp"], 1)


            def stream(b, u):
                wait(pool, s["xn2"], b - 1)
                wait(pool, s["x2b"], b - 1)
                landed(pool, l_y, b, u)
                one = lambda t: t[u][:, :].rearrange("p (o d) -> p o d", o=1)
                nc.gpsimd.tensor_tensor(one(x2), X[:, bass.ds(b, 1), :], one(y), ALU.add).then_inc(s["x2"], 1)

            def with_bias(b, u):
                pool.wait_ge(s["x2"], b + 1)
                wait(pool, s["x3"], b - 1)
                nc.gpsimd.tensor_tensor(x2b[u][:, :], x2[u][:, :], bo1[:, :], ALU.add).then_inc(s["x2b"], 1)

            def inv_std(x):
                mv, ve, r, ready, mid, done, used = x

                def stage(b, u):
                    pool.wait_ge(s[ready], b + 1)
                    wait(pool, s[used], b - 1)
                    nc.gpsimd.tensor_tensor(ve[u][:, :], mv[u][:, 1:2], eps[:, :], ALU.add).then_inc(s[mid], 1)
                    pool.wait_ge(s[mid], b + 1)
                    nc.gpsimd.tensor_tensor(r[u][:, :], ve[u][:, :], power[:, 0:1], ALU.pow).then_inc(s[done], 1)
                return stage

            inv2 = inv_std((mv2, v2e, r2, "mv2", "v2", "r2", "xn2"))
            inv3 = inv_std((mv3, v3e, r3, "mv3", "v3", "r3", "xn3"))

            def total(b, u):
                pool.wait_ge(s["pk"], 2 * b + 2)
                nc.gpsimd.tensor_tensor(sum4[u][:, :, :], picked[u][:, 0:4, :], picked[u][:, 4:8, :], ALU.add).then_inc(s["s4"], 1)
                pool.wait_ge(s["s4"], b + 1)
                nc.gpsimd.tensor_tensor(sum4[u][:, 0:2, :], sum4[u][:, 0:2, :], sum4[u][:, 2:4, :], ALU.add).then_inc(s["s2"], 1)
                pool.wait_ge(s["s2"], b + 1)
                nc.gpsimd.tensor_tensor(sum4[u][:, 0, :], sum4[u][:, 0, :], sum4[u][:, 1, :], ALU.add).then_inc(s["s1"], 1)
                pool.wait_ge(s["s1"], b + 1)
                pool.wait_ge(s["x3b"], b + 1)
                free(pool, st_o, b, u)
                nc.gpsimd.tensor_tensor(res[u][:, :], sum4[u][:, 0, :], x3b[u][:, :], ALU.add).then_inc(s["res"], 1)

            pipeline(pool, B, [
                (total, 6), (inv3, 4), (with_bias, 2), (inv2, 1), (keys, 1), (stream, 0), (values, 1)])

        @block.sync
        def _(sp):
            def load(b, u):
                wait(sp, s["x2"], b - 1)
                sp.dma_start(y[u][:, :], routed[SPARE:SPARE + B * S].rearrange("(b p) d -> b p d", b=B)[bass.ds(b, 1)]
                             .rearrange("o p d -> (o p) d")).then_inc(l_y[u], 16)

            def store(b, u):
                sp.wait_ge(s["res"], b + 1)
                sp.dma_start(out[bass.ds(b, 1)].rearrange("o s d -> (o s) d"), res[u][:, :]).then_inc(st_o[u], 16)

            pipeline(sp, B, [(load, 0), (store, 8)])
            for u in two:
                sp.wait_ge(st_o[u], 8 * B)


def kernel(**inputs):
    import concourse.bacc as _bacc
    from concourse.bass_utils import run_bass_kernel_spmd as _run

    def i(name):
        return np.asarray(inputs[name])

    table = i("L1_xattn_bias_table").T
    arrays = {
        "x": i("x"),
        "ctxT": i("ctx_1024").transpose(2, 0, 1).reshape(D, NG, PAIR * SK),
        "mask": i("mask_BxSxS2_ik1").transpose(1, 0, 2),
        "wqT0": i("L0_xattn_Wq").T, "wkT0": i("L0_xattn_Wk").T, "wv0": i("L0_xattn_Wv"), "wv1": i("L1_xattn_Wv"),
        "bq0": i("L0_xattn_bq"), "bk0": i("L0_xattn_bk"), "bv0": i("L0_xattn_bv"),
        "gamma": i("L0_xattn_ln_gamma"), "beta": i("L0_xattn_ln_beta"),
        "bq1": i("L1_xattn_bq"), "bk1": i("L1_xattn_bk"), "bv1": i("L1_xattn_bv"), "bo1": i("L1_xattn_bo"),
        "g_xattn": i("g_xattn"), "g_ffn": i("g_ffn"),
        "logit_scale": np.repeat(i("L1_xattn_logit_scale"), HD),
        "wk1": i("L1_xattn_Wk"), "wq1": i("L1_xattn_Wq"), "wo1": i("L1_xattn_Wo"),
        "router": i("L0_ffn_router").T, "wgs": i("L0_ffn_w_gate_s").T, "wus": i("L0_ffn_w_up_s").T,
        "wds": i("L0_ffn_w_down_s").T.reshape(HC, 128, D).transpose(1, 0, 2),
        "wgu": np.concatenate([i("L0_ffn_gate"), i("L0_ffn_up")], axis=1).transpose(2, 0, 1),
        "wdn": i("L0_ffn_down").transpose(2, 0, 1).reshape(HC, 128, E, D).transpose(1, 2, 0, 3).reshape(128, E, HC * D),
        "sigs": i("L1_ffn_tile_sigs").T, "w2": i("L1_ffn_W").transpose(1, 0, 2), "b2": i("L1_ffn_b"),
        "pad": i("mask_BxS2_bf0").reshape(-1),
        "table": table,
        "cst": constants(),
    }
    nc = _bacc.Bacc("TRN2", target_bir_lowering=False, num_devices=1)
    feed, aps = {}, {}
    for name, v in arrays.items():
        feed[f"in_{name}"] = np.ascontiguousarray(v)
        aps[name] = nc.dram_tensor(f"in_{name}", v.shape, mybir.dt.from_np(v.dtype), kind="ExternalInput").ap()
    out = nc.dram_tensor("out_0", (B, S, D), F32, kind="ExternalOutput").ap()
    build(nc, aps, out)
    return _run(nc, [feed], core_ids=[0]).results[0]["out_0"]
```
